# Optimizing a Trainium2 kernel written in Bass

```python
import numpy as np
import jax
import jax.numpy as jnp

def _softmax(x, axis=-1):
    return jax.nn.softmax(x, axis=axis)

def _gelu(x):
    return jax.nn.gelu(x, approximate=True)

def _silu(x):
    return jax.nn.silu(x)

def _sigmoid(x):
    return jax.nn.sigmoid(x)

def _layernorm(x, axis=-1, eps=1e-05):
    m = jnp.mean(x, axis=axis, keepdims=True)
    v = jnp.var(x, axis=axis, keepdims=True)
    return (x - m) / jnp.sqrt(v + eps)

def _scatter_add(tgt, idx, src, axis=0):
    return tgt.at[idx].add(src)

def _segment_sum(src, seg, n):
    return jax.ops.segment_sum(src, seg, n)
kernel_name = 'mk_flamingo_gated_d1_seqx_r4_0db451'

def setup_inputs(seed: int=0):
    np.random.seed(seed)
    _w = jnp.asarray

    def _rec_inputs():
        import jax
        import jax.numpy as jnp
        _rk = jax.random.key(seed)
        x = -0.0003929 + 0.9999 * jax.random.normal(jax.random.fold_in(_rk, 1), (4, 1024, 256), jnp.float32)
        _lenS = 1024 - jax.random.randint(jax.random.fold_in(_rk, 7), (4,), 0, max(1, 1024 // 4) + 1, jnp.int32)
        _lenS2 = 77 - jax.random.randint(jax.random.fold_in(_rk, 8), (4,), 0, max(1, 77 // 4) + 1, jnp.int32)
        _ctx_1024P = jax.random.normal(jax.random.fold_in(_rk, 11), (4, 16, 256), jnp.float32)
        _ctx_1024c = jax.random.dirichlet(jax.random.fold_in(_rk, 511), 0.3 * jnp.ones((16,), jnp.float32), (4, 77))
        _ctx_1024t = jnp.einsum('bsk,bkd->bsd', _ctx_1024c, _ctx_1024P)
        _ctx_1024t = _ctx_1024t * jax.lax.rsqrt(jnp.mean(jnp.square(_ctx_1024t)) + 1e-12) * 0.953939
        ctx_1024 = -0.000514642 + 1.00011 * (_ctx_1024t + 0.3 * jax.random.normal(jax.random.fold_in(_rk, 611), (4, 77, 256), jnp.float32))
        itok_BxS_0_511 = jax.random.randint(jax.random.fold_in(_rk, 12), (4, 1024), 0, 128, jnp.int32)
        _g = jax.random.normal(jax.random.fold_in(_rk, 9001), (2, 1), jnp.float32)
        _g = jnp.sign(_g) * jnp.maximum(jnp.abs(_g), 1.0) + (_g == 0) * 1.0
        g_xattn = _g[0]
        g_ffn = _g[1]
        return (x, ctx_1024, itok_BxS_0_511, g_xattn, g_ffn)
    x, ctx_1024, itok_BxS_0_511, g_xattn, g_ffn = _rec_inputs()

    def _L0_xattn_setup():
        import jax, jax.numpy as jnp
        import numpy as np
        Q_DIM = 256
        KV_DIM = 256
        D_ATTN = 256
        N_HEADS = 16
        HDIM = D_ATTN // N_HEADS
        LOOKBACK = 3
        KW = LOOKBACK + 1
        SCALE = HDIM ** (-0.5)
        B, LQ, LKV = (4, 1024, 128)

        def _split_heads(x):
            b, l, _ = x.shape
            return x.reshape(b, l, N_HEADS, HDIM).transpose(0, 2, 1, 3)
        key = jax.random.key(seed)
        ks = jax.random.split(key, 6)
        q = jax.random.normal(ks[0], (B, LQ, Q_DIM), dtype=jnp.float32)
        kv_src = jax.random.normal(ks[1], (B, LKV, KV_DIM), dtype=jnp.float32)
        seg_id = jnp.sort(jax.random.randint(ks[2], (B, LQ), 0, LKV), axis=-1)
        Wq = jax.random.normal(ks[3], (D_ATTN, Q_DIM), dtype=jnp.float32) * Q_DIM ** (-0.5)
        Wkv = jax.random.normal(ks[4], (2 * D_ATTN, KV_DIM), dtype=jnp.float32) * KV_DIM ** (-0.5)
        Wo = jax.random.normal(ks[5], (Q_DIM, D_ATTN), dtype=jnp.float32) * D_ATTN ** (-0.5)
        return {'q': q, 'kv_src': kv_src, 'seg_id': seg_id, 'Wq': Wq, 'Wkv': Wkv, 'Wo': Wo}
    _L0_xattn_all = _L0_xattn_setup()
    _L0_xattn_in = {k: v for k, v in _L0_xattn_all.items() if k in ('Wq', 'Wkv', 'Wo')}
    del _L0_xattn_all

    def _L0_ffn_setup():
        import jax, jax.numpy as jnp
        import numpy as np

        def _ste(w, w_q):
            return w + jax.lax.stop_gradient(w_q - w)

        def quantize_w8_per(w, axis):
            amax = jnp.clip(jnp.max(jnp.abs(w), axis=axis, keepdims=True), 1e-08, None)
            scale = 127.0 / amax
            w_q = jnp.clip(jnp.round(w * scale), -128.0, 127.0) / scale
            return _ste(w, w_q)

        def quantize_a16(x):
            amax = jnp.clip(jnp.max(jnp.abs(x)), 1e-08, None)
            scale = 32767.0 / amax
            x_q = jnp.clip(jnp.round(x * scale), -32768.0, 32767.0) / scale
            return _ste(x, x_q)
        key = jax.random.key(seed)
        k1, k2, k3 = jax.random.split(key, 3)
        d_model, d_ff = (256, 1024)
        x = jax.random.normal(k1, (4, 512, d_model), dtype=jnp.float32)
        W_in = jax.random.normal(k2, (d_model, d_ff), dtype=jnp.float32) / np.sqrt(d_model)
        b_in = jnp.zeros((d_ff,), dtype=jnp.float32)
        W_out = jax.random.normal(k3, (d_ff, d_model), dtype=jnp.float32) / np.sqrt(d_ff)
        b_out = jnp.zeros((d_model,), dtype=jnp.float32)
        return {'x': x, 'W_in': W_in, 'b_in': b_in, 'W_out': W_out, 'b_out': b_out}
    _L0_ffn_all = _L0_ffn_setup()
    _L0_ffn_in = {k: v for k, v in _L0_ffn_all.items() if k in ('W_in', 'b_in', 'W_out', 'b_out')}
    del _L0_ffn_all
    return {'x': x, 'ctx_1024': ctx_1024, 'itok_BxS_0_511': itok_BxS_0_511, 'g_xattn': g_xattn, 'g_ffn': g_ffn, 'L0_xattn_Wq': _L0_xattn_in['Wq'], 'L0_xattn_Wkv': _L0_xattn_in['Wkv'], 'L0_xattn_Wo': _L0_xattn_in['Wo'], 'L0_ffn_W_in': _L0_ffn_in['W_in'], 'L0_ffn_b_in': _L0_ffn_in['b_in'], 'L0_ffn_W_out': _L0_ffn_in['W_out'], 'L0_ffn_b_out': _L0_ffn_in['b_out']}

def reference(x, ctx_1024, itok_BxS_0_511, g_xattn, g_ffn, L0_xattn_Wq, L0_xattn_Wkv, L0_xattn_Wo, L0_ffn_W_in, L0_ffn_b_in, L0_ffn_W_out, L0_ffn_b_out):
    import jax
    import jax.numpy as jnp

    def _L0_xattn_ref(q, kv_src, seg_id, Wq, Wkv, Wo):
        import jax, jax.numpy as jnp
        import numpy as np
        Q_DIM = 256
        KV_DIM = 256
        D_ATTN = 256
        N_HEADS = 16
        HDIM = D_ATTN // N_HEADS
        LOOKBACK = 3
        KW = LOOKBACK + 1
        SCALE = HDIM ** (-0.5)
        B, LQ, LKV = (4, 1024, 128)

        def _split_heads(x):
            b, l, _ = x.shape
            return x.reshape(b, l, N_HEADS, HDIM).transpose(0, 2, 1, 3)
        b, lq, _ = q.shape
        lkv = kv_src.shape[1]
        qh = _split_heads(q @ Wq.T)
        kv = kv_src @ Wkv.T
        k, v = jnp.split(kv, 2, axis=-1)
        kh = _split_heads(k)
        vh = _split_heads(v)
        offsets = jnp.arange(KW)
        gather = seg_id[:, :, None] - offsets
        neg_mask = gather < 0
        gc = jnp.clip(gather, 0, lkv - 1)
        b_idx = jnp.arange(b)[:, None, None]
        k_sel = kh[b_idx, :, gc].transpose(0, 3, 1, 2, 4)
        v_sel = vh[b_idx, :, gc].transpose(0, 3, 1, 2, 4)
        scores = jnp.einsum('bhqd,bhqkd->bhqk', qh, k_sel) * SCALE
        neg_inf = jnp.finfo(scores.dtype).min
        scores = jnp.where(neg_mask[:, None, :, :], neg_inf, scores)
        probs = jax.nn.softmax(scores, axis=-1)
        out = jnp.einsum('bhqk,bhqkd->bhqd', probs, v_sel)
        out = out.transpose(0, 2, 1, 3).reshape(b, lq, D_ATTN)
        return out @ Wo.T

    def _L0_ffn_ref(x, W_in, b_in, W_out, b_out):
        import jax, jax.numpy as jnp
        import numpy as np

        def _ste(w, w_q):
            return w + jax.lax.stop_gradient(w_q - w)

        def quantize_w8_per(w, axis):
            amax = jnp.clip(jnp.max(jnp.abs(w), axis=axis, keepdims=True), 1e-08, None)
            scale = 127.0 / amax
            w_q = jnp.clip(jnp.round(w * scale), -128.0, 127.0) / scale
            return _ste(w, w_q)

        def quantize_a16(x):
            amax = jnp.clip(jnp.max(jnp.abs(x)), 1e-08, None)
            scale = 32767.0 / amax
            x_q = jnp.clip(jnp.round(x * scale), -32768.0, 32767.0) / scale
            return _ste(x, x_q)
        W_in_sim = quantize_w8_per(W_in, axis=0)
        W_out_sim = quantize_w8_per(W_out, axis=1)
        x_sim = quantize_a16(x)
        hidden = jax.nn.gelu(x_sim @ W_in_sim + b_in, approximate=False)
        hidden_sim = quantize_a16(hidden)
        out = hidden_sim @ W_out_sim + b_out
        return out
    x = x + jnp.tanh(g_xattn[0]) * _L0_xattn_ref(_layernorm(x, axis=-1), ctx_1024, itok_BxS_0_511, L0_xattn_Wq, L0_xattn_Wkv, L0_xattn_Wo)
    x = x + jnp.tanh(g_ffn[0]) * _L0_ffn_ref(_layernorm(x, axis=-1), L0_ffn_W_in, L0_ffn_b_in, L0_ffn_W_out, L0_ffn_b_out)
    return x

_drawn_inputs = setup_inputs


def setup_inputs(seed=0):
    import zlib

    import numpy as np

    out = dict(_drawn_inputs(seed))
    spreads = {'L0_ffn_b_in': (0.0, 0.1), 'L0_ffn_b_out': (0.0, 0.1)}
    factors = {}
    for name, (base, spread) in spreads.items():
        noise = np.random.default_rng([zlib.crc32(name.encode()), seed]).standard_normal(out[name].shape)
        drawn = base * np.exp(spread * noise) if base else spread * noise
        out[name] = jnp.asarray(drawn.astype(out[name].dtype))
    for name, factor in factors.items():
        out[name] = (out[name] * factor).astype(out[name].dtype)
    return out
```

```python
from contextlib import ExitStack

import concourse.bass as bass
from concourse import mybir

P = 128
ALU = mybir.AluOpType
ACT = mybir.ActivationFunctionType
AX = mybir.AxisListType
F32 = mybir.dt.float32
F16 = mybir.dt.float16
BF16 = mybir.dt.bfloat16
I16 = mybir.dt.int16
I32 = mybir.dt.int32
RMAX = bass.bass_isa.ReduceOp.max

LN_EPS = 1e-5
AMAX_FLOOR = 1e-8
W_LEVELS = 127.0
A_LEVELS = 32767.0
NEG = -3.4028234663852886e38
POW2_BITS = 0x7F800000
HALF_TOP = 16384.0


def flamingo_kernel(nc, x, ctx_kv, seg, g_xattn, g_ffn, w_q, w_kv, w_o, w_in, b_in, w_out, b_out, out):
    NB, LQ, D = x.shape
    LKV = ctx_kv.shape[1]
    F = w_in.shape[1]
    H, HD = 16, D // 16
    KW = 4
    U = LKV + KW - 1
    C = D // P
    FC = F // P
    TB = LQ // P
    NT = NB * TB
    NP = NT // 2
    NG = NT // 4
    GT = 4 * P
    SCALE = float(HD) ** -0.5

    with ExitStack() as ctx:
        def sem(name):
            return ctx.enter_context(nc.semaphore(name))

        base = (nc.sbuf_base + 63) // 64 * 64
        size = {F32: 4, I32: 4, F16: 2, BF16: 2, I16: 2}

        class Region:
            def __init__(self, start, length):
                self.at, self.end = start, start + length

            def put(self, name, shape, dt):
                n = size[dt]
                for d in shape[1:]:
                    n *= d
                off = (self.at + 31) // 32 * 32
                self.at = off + n
                assert self.at <= self.end, (name, self.at - self.end)
                return nc.alloc_sbuf_tensor_at(name, shape, dt, offset=off)

        HID = FC * GT * 4 * NG
        SLOT = HID // NG
        XN2T = C * NT * P * 4
        RES = NT * D * 4
        hid_r = Region(base, HID)
        a_r = Region(base, HID - XN2T)
        x2_r = Region(base + HID - XN2T, XN2T)
        pre_r = Region(base + HID - XN2T, XN2T)
        keep_r = Region(base + HID, RES + 12800)
        bc_r = Region(base + HID + RES + 12800, nc.sbuf_usable_end - (base + HID + RES + 12800))
        pre2_r = Region(base + HID + RES + 12800, nc.sbuf_usable_end - (base + HID + RES + 12800))

        hidden = hid_r.put("hidden", [P, NG, FC, GT], F32)
        xn2T = x2_r.put("xn2T", [P, NG, C, GT], F32)

        xres = keep_r.put("xres", [P, NT, D], F32)
        win8 = keep_r.put("win8", [P, C, F], F16)
        wout8 = keep_r.put("wout8", [P, FC, D], F16)
        ident = keep_r.put("ident", [P, P], F32)
        ident16 = keep_r.put("ident16", [P, P], F16)
        neg = keep_r.put("neg", [P, NT, KW], F32)
        bout = keep_r.put("bout", [P, D], F32)
        bin_ = keep_r.put("bin_", [P, FC], F32)
        bin_ld = keep_r.put("bin_ld", [FC, P], F32)
        gates = keep_r.put("gates", [P, 2], F32)
        tanhs = keep_r.put("tanhs", [P, 2], F32)
        amax_win = keep_r.put("amax_win", [P, FC], F32)
        amax_wout = keep_r.put("amax_wout", [P, FC], F32)
        sc_win = keep_r.put("sc_win", [P, FC], F32)
        sc_wout = keep_r.put("sc_wout", [P, FC], F32)
        rel_wout = keep_r.put("rel_wout", [P, FC], F32)
        top_wout = keep_r.put("top_wout", [P, 3], F32)
        zscale = keep_r.put("zscale", [P, FC], F32)
        qx = keep_r.put("qx", [P, 8], F32)
        qh = keep_r.put("qh", [P, 8], F32)
        hmax = keep_r.put("hmax", [P, NG * FC // 2], F32)
        xmax = keep_r.put("xmax", [P, NP], F32)
        consts = keep_r.put("consts", [P, 8], F32)

        onehot = a_r.put("onehot", [U, KW, NT * P], BF16)
        kvtab = a_r.put("kvtab", [U, NB, 2, 2 * D], F16)
        wqT = a_r.put("wqT", [P, C, D], F32)
        woT = a_r.put("woT", [P, C, D], F32)

        def pair(name, shape, dt=F32):
            return [a_r.put(f"{name}{i}", shape, dt) for i in range(2)]

        xn, xT, q = pair("xn", [P, 2, D]), pair("xT", [P, C, 2 * P]), pair("q", [P, 2, D])
        prod, vsel = pair("prod", [P, KW, D]), pair("vsel", [P, KW, D])
        o, oT, xn2 = pair("o", [P, 2, D]), pair("oT", [P, C, 2 * P]), pair("xn2", [P, 2, D])
        s, e, pr = pair("s", [P, 2, KW, H]), pair("e", [P, 2, KW, H]), pair("pr", [P, 2, KW, H])
        smax, ssum, srec = pair("smax", [P, 2, H]), pair("ssum", [P, 2, H]), pair("srec", [P, 2, H])
        bn = [pair("bn1_", [P, 2, 6]), pair("bn2_", [P, 2, 6])]
        mv = [pair("mv1_", [P, 2, 2]), pair("mv2_", [P, 2, 2])]
        ve = [pair("ve1_", [P, 2]), pair("ve2_", [P, 2])]
        rstd = [pair("rstd1_", [P, 2]), pair("rstd2_", [P, 2])]
        ctxT = a_r.put("ctxT", [P, C, NB * U], F32)
        wkvT = pre2_r.put("wkvT", [P, C, 2 * D], F32)

        seg_i = pre_r.put("seg_i", [U, NB * LQ], I32)
        seg_b = pre_r.put("seg_b", [U, NB * LQ], BF16)
        wkv_ld = pre_r.put("wkv_ld", [P, 2 * C, D], F32)
        ctx_ld = pre_r.put("ctx_ld", [U, NB, D], F32)
        wq_ld = pre2_r.put("wq_ld", [P, C, D], F32)
        wo_ld = pre2_r.put("wo_ld", [P, C, D], F32)
        win_ld = pre2_r.put("win_ld", [P, C, F], F32)
        wout_ld = pre2_r.put("wout_ld", [P, FC, D], F32)
        w_i16 = pre2_r.put("w_i16", [P, FC, D], I16)
        win_f16 = pre2_r.put("win_f16", [P, FC, D], F16)
        seg_t = keep_r.put("seg_t", [P, NT], I32)
        seg_f = keep_r.put("seg_f", [P, NT], F32)
        jo = keep_r.put("jo", [U, KW], F32)
        kvp = keep_r.put("kvp", [U, 4, NB], F32)

        xr = [bc_r.put(f"xr{i}", [P, C, GT], I16) for i in range(2)]
        xhi = [bc_r.put(f"xhi{i}", [P, C, GT], F16) for i in range(2)]
        xlo = [bc_r.put(f"xlo{i}", [P, C, GT], F16) for i in range(2)]
        hq = [bc_r.put(f"hq{i}", [P, 2, GT], I16) for i in range(2)]
        hhi = [bc_r.put(f"hhi{i}", [P, GT], F16) for i in range(4)]
        hlo = [bc_r.put(f"hlo{i}", [P, GT], F16) for i in range(4)]
        y = [bc_r.put(f"y{i}", [P, 4, D], F32) for i in range(2)]

        bank01 = ctx.enter_context(nc.psum_tensor("bank01", [P, 1024], F32))
        bank23 = ctx.enter_context(nc.psum_tensor("bank23", [P, 1024], F32))
        bank45 = ctx.enter_context(nc.psum_tensor("bank45", [P, 1024], F32))
        bank67 = ctx.enter_context(nc.psum_tensor("bank67", [P, 1024], F32))
        wide = [bank01, bank23, bank45, bank67]
        ps_k, ps_v = bank01, bank23
        ps_t, ps_q = bank45[:, 0:512], bank45[:, 512:1024]
        ps_o, ps_y = bank67[:, 0:512], bank67[:, 512:1024]

        s_x = [sem(f"x_loaded{b}") for b in range(NB)]
        s_ctx, s_wkv, s_segb, s_segt = sem("ctx_loaded"), sem("wkv_loaded"), sem("segb_loaded"), sem("segt_loaded")
        s_wq, s_wo, s_win, s_wout = sem("wq_loaded"), sem("wo_loaded"), sem("win_loaded"), sem("wout_loaded")
        s_small = sem("small_loaded")
        s_ident0, s_ident, s_jo = sem("ident_zeroed"), sem("ident_ready"), sem("jo_ready")
        s_const = sem("consts_ready")
        s_segc = sem("segb_clamped")
        s_ctxTp, s_ctxT, s_wkvTp, s_wkvT = sem("ctxT_in_psum"), sem("ctxT_ready"), sem("wkvT_in_psum"), sem("wkvT_ready")
        s_wqTp, s_wqT, s_woTp, s_woT = sem("wqT_in_psum"), sem("wqT_ready"), sem("woT_in_psum"), sem("woT_ready")
        s_kv, s_kvscale, s_kvhi, s_kvlo = sem("kv_in_psum"), sem("kv_scales"), sem("kv_hi_ready"), sem("kv_lo_ready")
        s_oh, s_neg = sem("onehot_ready"), sem("neg_ready")
        s_winTp, s_winq, s_w8p, s_w8 = sem("winT_in_psum"), sem("win_quantised"), sem("win8_in_psum"), sem("win8_ready")
        s_wout8 = sem("wout8_ready")
        s_tanh = sem("tanh_ready")
        s_vc = sem("vector_setup_chain")
        s_bn = [sem("stats1_parts"), sem("stats2_parts")]
        s_mv = [sem("stats1_ready"), sem("stats2_ready")]
        s_ve = [sem("var1_eps"), sem("var2_eps")]
        s_rstd = [sem("rstd1_ready"), sem("rstd2_ready")]
        s_xn, s_xTp, s_xT = sem("xn_ready"), sem("xT_in_psum"), sem("xT_ready")
        s_qp, s_q = sem("q_in_psum"), sem("q_ready")
        s_kp, s_prod, s_red = sem("k_in_psum"), sem("qk_products"), sem("scores_summed")
        s_masked, s_smax, s_shift = sem("scores_masked"), sem("score_max"), sem("scores_shifted")
        s_exp, s_ssum, s_srec, s_p = sem("exp_ready"), sem("exp_sum"), sem("exp_sum_inv"), sem("probs_ready")
        s_vp, s_vc2 = sem("v_in_psum"), sem("v_copied")
        s_pv, s_pv2, s_o = sem("pv_products"), sem("pv_halves"), sem("o_tile_ready")
        s_oTp, s_oT, s_yp, s_x1 = sem("oT_in_psum"), sem("oT_ready"), sem("attn_out_in_psum"), sem("x1_ready")
        s_xn2, s_xn2Tp, s_xn2T = sem("xn2_ready"), sem("xn2T_in_psum"), sem("xn2T_ready")
        s_xmax = sem("xn2_max")
        s_pace = [sem("pace_vector"), sem("pace_scalar")]
        s_xall, s_qxr, s_qxs = sem("x_amax_row"), sem("x_amax_all"), sem("x_scale_ready")
        s_qxc = sem("x_scale_chain")
        s_bias = sem("bout_scaled")
        s_xr, s_xhi, s_xq = sem("x_rounded"), sem("x_hi_ready"), sem("x_quantised")
        s_z, s_h, s_hm = sem("z_in_psum"), sem("hidden_ready"), sem("hidden_pair_max")
        s_hall, s_qhr, s_qhc, s_qhs = sem("h_amax_row"), sem("h_amax_all"), sem("h_scale_chain"), sem("h_scale_ready")
        s_wrow, s_wall = sem("wout_amax_row"), sem("wout_amax_all")
        s_x1b = sem("x1_with_bias")
        s_hq, s_hhi, s_hlo = sem("hidden_rounded"), sem("hidden_hi_ready"), sem("hidden_lo_ready")
        s_hused, s_acc, s_ys, s_out = sem("hidden_chunk_used"), sem("out_in_psum"), sem("out_scaled"), sem("out_ready")
        s_stored = [sem("stored_even"), sem("stored_odd")]

        x_d = x.rearrange("b (p t) d -> b p t d", p=P)
        out_d = out.rearrange("b (p t) d -> b p t d", p=P)
        kv_ap = [(bank01, 0), (bank01, 512), (bank23, 0), (bank23, 512)]
        win_half = [bank23, bank67]

        BIN_AT = NB * U

        def first(u, n):
            return not isinstance(u, int) or u >= n

        block = ctx.enter_context(nc.Block())

        @block.sync
        def _(sp):
            sp.dma_start(xres[:, 0:TB, :], x_d[0]).then_inc(s_x[0], 16)
            sp.dma_start(wkv_ld[:], w_kv.rearrange("(c p) d -> p c d", p=P)).then_inc(s_wkv, 16)
            sp.dma_start(wq_ld[:], w_q.rearrange("(c p) d -> p c d", p=P)).then_inc(s_wq, 16)
            sp.dma_start(seg_i[:], seg.rearrange("b n -> (b n)").partition_broadcast(U)).then_inc(s_segb, 16)
            sp.dma_start(win_ld[:], w_in.rearrange("(c p) f -> p c f", p=P)).then_inc(s_win, 16)
            sp.dma_start(wout_ld[:], w_out.rearrange("(c p) d -> p c d", p=P)).then_inc(s_wout, 16)
            for b in range(1, NB):
                sp.dma_start(xres[:, TB * b:TB * (b + 1), :], x_d[b]).then_inc(s_x[b], 16)
            for g in range(NG):
                b, t0 = g * 4 // TB, g * 4 % TB
                sp.wait_ge(s_out, g + 1)
                sp.dma_start(out_d[b, :, t0:t0 + 4, :], y[g % 2][:]).then_inc(s_stored[g % 2], 16)
            for k in range(2):
                sp.wait_ge(s_stored[k], 16 * (NG // 2))

        @block.gpsimd
        def _(pool):
            pool.memset(ident[:], 0.0).then_inc(s_ident0, 1)
            pool.memset(ident16[:], 0.0).then_inc(s_ident0, 1)
            pool.memset(consts[:, 0:2], LN_EPS).then_inc(s_const, 1)
            pool.memset(consts[:, 2:4], -0.5).then_inc(s_const, 1)
            pool.wait_ge(s_ident0, 2)
            for m in (ident, ident16):
                pool.affine_select(out=m[:], in_=m[:], compare_op=ALU.not_equal, fill=1.0, base=0,
                                   pattern=[[-1, P]], channel_multiplier=1).then_inc(s_ident, 1)
            pool.iota(jo[:], pattern=[[1, KW]], base=0, channel_multiplier=1,
                      allow_small_or_imprecise_dtypes=True).then_inc(s_jo, 1)
            pool.wait_ge(s_segb, 16)
            for b in range(NB):
                src = seg_i[:, b * LQ:(b + 1) * LQ].rearrange("u (p t) -> u t p", t=TB)
                dst = seg_b[:, b * LQ:(b + 1) * LQ].rearrange("u (t p) -> u t p", t=TB)
                pool.tensor_scalar(dst, src, float(U - 1), 0.0, ALU.min, ALU.max).then_inc(s_segc, 1)

            def inv_std(n, u, k):
                pool.wait_ge(s_mv[n], u + 1)
                pool.tensor_tensor(ve[n][k][:], mv[n][k][:, :, 1], consts[:, 0:2], ALU.add).then_inc(s_ve[n], 1)
                pool.wait_ge(s_ve[n], u + 1)
                pool.tensor_tensor(rstd[n][k][:], ve[n][k][:], consts[:, 2:4], ALU.pow).then_inc(s_rstd[n], 1)

            def weigh_v(u, k, t):
                n = 2 * u + t
                v4 = vsel[t][:].rearrange("p o (h d) -> p o h d", h=H)
                p4 = pr[k][:, t].unsqueeze(3).broadcast_to([P, KW, H, HD])
                pool.wait_ge(s_vc2, n + 1)
                pool.wait_ge(s_p, u + 1)
                pool.tensor_tensor(v4.rearrange("p o h d -> p (o h) d"), v4.rearrange("p o h d -> p (o h) d"),
                                   pr[k][:, t].rearrange("p o h -> p (o h)").unsqueeze(2).broadcast_to([P, KW * H, HD]),
                                   ALU.mult).then_inc(s_pv, 1)
                pool.wait_ge(s_pv, n + 1)
                pool.tensor_tensor(vsel[t][:, 0:2, :], vsel[t][:, 0:2, :], vsel[t][:, 2:4, :], ALU.add).then_inc(s_pv2, 1)
                pool.wait_ge(s_pv2, n + 1)
                if first(u, 2):
                    pool.wait_ge(s_oTp, u - 1)
                pool.tensor_tensor(o[k][:, t, :], vsel[t][:, 0, :], vsel[t][:, 1, :], ALU.add).then_inc(s_o, 1)

            def step(i, k):
                if not isinstance(i, int) or i < NP:
                    inv_std(0, i, k)
                v_on = not isinstance(i, int) or 2 <= i < NP + 2
                if v_on:
                    weigh_v(i - 2, k, 0)
                if not isinstance(i, int) or 3 <= i < NP + 3:
                    inv_std(1, i - 3, 1 - k)
                if v_on:
                    weigh_v(i - 2, k, 1)

            pool.wait_ge(s_const, 2)
            for i in range(6):
                step(i, i % 2)
            with pool.Fori(3, NP // 2) as j:
                for k in range(2):
                    step(2 * j + k, k)
            for i in range(NP, NP + 4):
                step(i, i % 2)

            pool.wait_ge(s_wrow, 1)
            pool.partition_all_reduce(top_wout[:, 1:2], top_wout[:, 0:1], P, RMAX).then_inc(s_wall, 1)
            pool.wait_ge(s_xall, 1)
            pool.partition_all_reduce(qx[:, 1:2], qx[:, 0:1], P, RMAX).then_inc(s_qxr, 1)
            pool.wait_ge(s_bias, 1)
            for g in range(NG):
                v = xres[:, 4 * g:4 * g + 4, :]
                pool.tensor_tensor(v, v, bout[:].unsqueeze(1).broadcast_to([P, 4, D]), ALU.add).then_inc(s_x1b, 1)
            pool.wait_ge(s_hall, 1)
            pool.partition_all_reduce(qh[:, 1:2], qh[:, 0:1], P, RMAX).then_inc(s_qhr, 1)
            pool.wait_ge(s_x1b, NG)

            def add_residual(g, k):
                pool.wait_ge(s_ys, 4 * g + 4)
                pool.tensor_tensor(y[k][:], y[k][:], xres[:, bass.ds(4 * g, 4), :], ALU.add).then_inc(s_out, 1)

            with pool.Fori(0, NG // 2) as j:
                for k in range(2):
                    add_residual(2 * j + k, k)

        @block.scalar
        def _(act):
            for b in range(NB):
                act.dma_start(ctx_ld[0:LKV, b, :], ctx_kv[b]).then_inc(s_ctx, 16)
                act.dma_start(ctx_ld[LKV:U, b, :], ctx_kv[b, LKV - 1, :].partition_broadcast(U - LKV)).then_inc(s_ctx, 16)
            act.dma_start(wo_ld[:], w_o.rearrange("(c p) d -> p c d", p=P)).then_inc(s_wo, 16)
            act.dma_start(seg_t[:].rearrange("p (b t) -> p b t", b=NB), seg.rearrange("b (p t) -> p b t", p=P)).then_inc(s_segt, 16)
            act.dma_start(gates[:, 0:1], g_xattn.partition_broadcast(P)).then_inc(s_small, 16)
            act.dma_start(gates[:, 1:2], g_ffn.partition_broadcast(P)).then_inc(s_small, 16)
            act.dma_start(bout[:], b_out.partition_broadcast(P)).then_inc(s_small, 16)
            act.dma_start(bin_ld[:], b_in.rearrange("(c p) -> c p", p=P)).then_inc(s_small, 16)

            def copy(dst, src):
                return act.activation(dst, src, ACT.Copy)

            act.wait_ge(s_ctxTp, 1)
            copy(ctxT[:], bank67[:].rearrange("p (c n) -> p c n", c=C)[:, :, 0:NB * U]).then_inc(s_ctxT, 1)
            copy(bin_[:], bank67[:, BIN_AT:BIN_AT + FC]).then_inc(s_ctxT, 1)
            act.wait_ge(s_wqTp, 1)
            copy(wqT[:].rearrange("p c d -> p (c d)"), ps_o).then_inc(s_wqT, 1)
            for b in range(NB):
                act.wait_ge(s_kvscale, 1)
                act.wait_ge(s_kv, NB)
                t, c0 = kv_ap[b]
                act.activation(kvtab[:, b, 0, :], t[0:U, c0:c0 + 2 * D], ACT.Copy, scale=kvp[:, 2, b:b + 1]).then_inc(s_kvhi, 1)
            act.wait_ge(s_woTp, 1)
            copy(woT[:].rearrange("p c d -> p (c d)"), ps_y).then_inc(s_woT, 1)
            act.wait_ge(s_small, 64)
            act.activation(tanhs[:], gates[:], ACT.Tanh).then_inc(s_tanh, 1)

            def evac_oT(u, k):
                act.wait_ge(s_oTp, u + 1)
                if first(u, 2):
                    act.wait_ge(s_yp, u - 1)
                copy(oT[k][:].rearrange("p c n -> p (c n)"), ps_o).then_inc(s_oT, 1)

            def copy_v(u, t):
                n = 2 * u + t
                act.wait_ge(s_vp, n + 1)
                if first(n, 2):
                    act.wait_ge(s_o, n - 1)
                copy(vsel[t][:].rearrange("p o d -> p (o d)"), ps_v[:]).then_inc(s_vc2, 1)

            def exp(u, k):
                act.wait_ge(s_shift, u + 1)
                act.activation(e[k][:].rearrange("p t o h -> p (t o h)"), s[k][:].rearrange("p t o h -> p (t o h)"),
                               ACT.Exp, scale=SCALE).then_inc(s_exp, 1)

            def evac_xn2T(u, k):
                act.wait_ge(s_xn2Tp, u + 1)
                if not isinstance(u, int):
                    act.sem_inc(s_pace[1], 1)
                copy(xn2T[:, u // 2, :, k * 2 * P:(k + 1) * 2 * P], ps_t.rearrange("p (c n) -> p c n", c=C)).then_inc(s_xn2T, 1)

            def evac_xT(u, k):
                act.wait_ge(s_xTp, u + 1)
                if first(u, 2):
                    act.wait_ge(s_qp, u - 1)
                copy(xT[k][:].rearrange("p c n -> p (c n)"), ps_t).then_inc(s_xT, 1)

            def evac_q(u, k):
                act.wait_ge(s_qp, u + 1)
                if first(u, 2):
                    act.wait_ge(s_prod, 2 * u - 2)
                copy(q[k][:].rearrange("p t d -> p (t d)"), ps_q).then_inc(s_q, 1)

            def step(i, k):
                on = lambda lag: not isinstance(i, int) or lag <= i < NP + lag
                if on(3):
                    evac_oT(i - 3, 1 - k)
                if on(2):
                    copy_v(i - 2, 0)
                    copy_v(i - 2, 1)
                if on(1):
                    exp(i - 1, 1 - k)
                if on(4):
                    evac_xn2T(i - 4, k)
                if on(0):
                    evac_xT(i, k)
                    evac_q(i, k)

            step(0, 0)
            step(1, 1)
            act.wait_ge(s_w8p, 1)
            copy(win8[:].rearrange("p c f -> p (c f)"), bank23[:].bitcast(F16)).then_inc(s_w8, 1)
            for i in range(2, 6):
                step(i, i % 2)
            with act.Fori(3, NP // 2) as j:
                for k in range(2):
                    step(2 * j + k, k)
            for i in range(NP, NP + 4):
                step(i, i % 2)

            act.wait_ge(s_qxs, 1)
            act.activation(qx[:, 6:7], consts[:, 0:1], ACT.Gelu)
            def gelu(g, k):
                for f in range(FC):
                    act.wait_ge(s_z, g * FC + f + 1)
                    if not isinstance(g, int):
                        act.sem_inc(s_pace[1], 1)
                    bank = wide[f // 2 % 4][:, (f % 2) * 512:(f % 2) * 512 + GT]
                    act.activation(hidden[:, g, f, :], bank, ACT.Gelu, bias=bin_[:, f:f + 1],
                                   scale=zscale[:, f:f + 1]).then_inc(s_h, 1)

            with act.Fori(0, NG) as g:
                gelu(g, 0)

            act.wait_ge(s_qhs, 1)

            def round_h(g, k):
                for m in range(FC // 2):
                    n = g * (FC // 2) + m
                    if first(n, 2):
                        act.wait_ge(s_hlo, 2 * n - 2)
                        if not isinstance(g, int):
                            act.sem_inc(s_pace[1], 1)
                    act.activation(hq[m % 2][:], hidden[:, g, 2 * m:2 * m + 2, :], ACT.Copy,
                                   scale=qh[:, 3:4]).then_inc(s_hq, 1)

            def scale_out(g, k):
                if first(g, 2):
                    act.wait_ge(s_stored[k], 8 * g - 8 * k)
                for t in range(4):
                    act.wait_ge(s_acc, g * 4 + t + 1)
                    bank = wide[2 * k + t // 2][:, (t % 2) * 512:(t % 2) * 512 + D]
                    act.activation(y[k][:, t, :], bank, ACT.Copy, scale=qh[:, 5:6]).then_inc(s_ys, 1)

            round_h(0, 0)
            for g in range(1, 4):
                round_h(g, g % 2)
                scale_out(g - 1, 1 - g % 2)
            with act.Fori(2, NG // 2) as j:
                for k in range(2):
                    round_h(2 * j + k, k)
                    scale_out(2 * j + k - 1, 1 - k)
            scale_out(NG - 1, 1)

        @block.tensor
        def _(pe):
            pe.wait_ge(s_ident, 2)
            pe.wait_ge(s_ctx, 16 * 2 * NB)
            for b in range(NB):
                for c in range(C):
                    mm = pe.transpose(bank67[:, c * 512 + b * U:c * 512 + (b + 1) * U], ctx_ld[:, b, c * P:(c + 1) * P],
                                      ident[0:U, 0:U])
            pe.wait_ge(s_small, 64)
            mm = pe.transpose(bank67[:, BIN_AT:BIN_AT + FC], bin_ld[:], ident[0:FC, 0:FC])
            mm.then_inc(s_ctxTp, 1)
            pe.wait_ge(s_wkv, 16)
            for r in range(2 * C):
                for c in range(C):
                    mm = pe.transpose(bank45[:, c * 512 + r * P:c * 512 + (r + 1) * P], wkv_ld[:, r, c * P:(c + 1) * P], ident[:])
            mm.then_inc(s_wkvTp, 1)

            def weight_T(dst, ld, landed, done):
                pe.wait_ge(landed, 16)
                for r in range(C):
                    for c in range(C):
                        mm = pe.transpose(dst[:, c * D + r * P:c * D + (r + 1) * P], ld[:, r, c * P:(c + 1) * P], ident[:])
                mm.then_inc(done, 1)

            pe.wait_ge(s_ctxT, 2)
            weight_T(ps_o, wq_ld, s_wq, s_wqTp)
            pe.wait_ge(s_wkvT, 1)
            for b in range(NB):
                t, c0 = kv_ap[b]
                for c in range(C):
                    mm = pe.matmul(t[0:U, c0:c0 + 2 * D], ctxT[:, c, b * U:(b + 1) * U], wkvT[:, c, :],
                                   start=(c == 0), stop=(c == C - 1))
                mm.then_inc(s_kv, 1)
            weight_T(ps_y, wo_ld, s_wo, s_woTp)

            def transpose_o(u, k):
                pe.wait_ge(s_o, 2 * u + 2)
                if first(u, 1):
                    pe.wait_ge(s_oT, u)
                for t in range(2):
                    for c in range(C):
                        mm = pe.transpose(ps_o[:, c * 2 * P + t * P:c * 2 * P + (t + 1) * P], o[k][:, t, c * P:(c + 1) * P], ident[:])
                mm.then_inc(s_oTp, 1)

            def gather(dst, col, u, t, done):
                tile = 2 * u + t
                b = u // (TB // 2)
                for off in range(KW):
                    for part in range(2):
                        mm = pe.matmul(dst[:, off * D:(off + 1) * D],
                                       onehot[:, off, bass.ds(tile * P, P)], kvtab[:, b, part, col:col + D],
                                       start=(part == 0), stop=(part == 1))
                mm.then_inc(done, 1)

            def gather_k(u, t):
                n = 2 * u + t
                if first(n, 1):
                    pe.wait_ge(s_prod, n)
                gather(ps_k, 0, u, t, s_kp)

            def gather_v(u, t):
                n = 2 * u + t
                if first(n, 1):
                    pe.wait_ge(s_vc2, n)
                gather(ps_v, D, u, t, s_vp)

            def project(dst, src, w, done):
                for t in range(2):
                    for c in range(C):
                        mm = pe.matmul(dst[:, t * D:(t + 1) * D], src[:, c, t * P:(t + 1) * P], w[:, c, :],
                                       start=(c == 0), stop=(c == C - 1))
                mm.then_inc(done, 1)

            def attn_out(u, k):
                pe.wait_ge(s_oT, u + 1)
                if first(u, 1):
                    pe.wait_ge(s_x1, u)
                project(ps_y, oT[k], woT, s_yp)

            def transpose_xn2(u, k):
                pe.wait_ge(s_xn2, u + 1)
                if isinstance(u, int) and u + 4 > NP:
                    pe.wait_ge(s_xn2T, u)
                else:
                    pe.wait_ge(s_xT, u + 4)
                for t in range(2):
                    for c in range(C):
                        mm = pe.transpose(ps_t[:, c * 2 * P + t * P:c * 2 * P + (t + 1) * P], xn2[k][:, t, c * P:(c + 1) * P], ident[:])
                mm.then_inc(s_xn2Tp, 1)

            def transpose_x(u, k):
                pe.wait_ge(s_xn, u + 1)
                if first(u, 4):
                    pe.wait_ge(s_xn2T, u - 3)
                elif u:
                    pe.wait_ge(s_xT, u)
                for t in range(2):
                    for c in range(C):
                        mm = pe.transpose(ps_t[:, c * 2 * P + t * P:c * 2 * P + (t + 1) * P], xn[k][:, t, c * P:(c + 1) * P], ident[:])
                mm.then_inc(s_xTp, 1)

            def queries(u, k):
                pe.wait_ge(s_xT, u + 1)
                if first(u, 1):
                    pe.wait_ge(s_q, u)
                project(ps_q, xT[k], wqT, s_qp)

            def step(i, k):
                on = lambda lag: not isinstance(i, int) or lag <= i < NP + lag
                if on(3):
                    transpose_o(i - 3, 1 - k)
                if on(1):
                    gather_k(i - 1, 0)
                if on(3):
                    attn_out(i - 3, 1 - k)
                if on(2):
                    gather_v(i - 2, 0)
                if on(1):
                    gather_k(i - 1, 1)
                if on(2):
                    gather_v(i - 2, 1)
                if on(4):
                    transpose_xn2(i - 4, k)
                if on(0):
                    transpose_x(i, k)
                    queries(i, k)

            pe.wait_ge(s_wqT, 1)
            step(0, 0)
            pe.wait_ge(s_win, 16)
            pe.wait_ge(s_kvhi, NB)
            pe.wait_ge(s_kvlo, NB)
            pe.wait_ge(s_woT, 1)
            for hf in range(2):
                for f in range(FC // 2):
                    for c in range(C):
                        fc = hf * (FC // 2) + f
                        mm = pe.transpose(win_half[hf][:, f * D + c * P:f * D + (c + 1) * P], win_ld[:, c, fc * P:(fc + 1) * P], ident[:])
                mm.then_inc(s_winTp, 1)
            pe.wait_ge(s_oh, NB)
            step(1, 1)
            pe.wait_ge(s_winq, 1)
            w8p = bank23[:].bitcast(F16).rearrange("p (c f) -> p c f", c=C)
            for f in range(FC):
                for c in range(C):
                    mm = pe.transpose(w8p[:, c, f * P:(f + 1) * P], win_f16[:, f, c * P:(c + 1) * P], ident16[:])
            mm.then_inc(s_w8p, 1)
            pe.wait_ge(s_w8, 1)
            for i in range(2, 6):
                step(i, i % 2)
            with pe.Fori(3, NP // 2) as j:
                for k in range(2):
                    step(2 * j + k, k)
            for i in range(NP, NP + 4):
                step(i, i % 2)

            pe.wait_ge(s_xn2T, NP)

            def expand(g, k):
                pe.wait_ge(s_xq, g + 1)
                for f in range(FC):
                    n = g * FC + f
                    if first(n, FC):
                        pe.wait_ge(s_h, g * FC + f - FC + 1)
                    bank = wide[f // 2 % 4][:, (f % 2) * 512:(f % 2) * 512 + GT]
                    at = 0
                    for c in range(C):
                        for part in (xhi, xlo):
                            mm = pe.matmul(bank, win8[:, c, f * P:(f + 1) * P], part[k][:, c, :],
                                           start=(at == 0), stop=(at == 2 * C - 1))
                            at += 1
                    mm.then_inc(s_z, 1)

            expand(0, 0)
            expand(1, 1)
            with pe.Fori(1, NG // 2) as j:
                for k in range(2):
                    expand(2 * j + k, k)

            pe.wait_ge(s_h, NG * FC)
            pe.wait_ge(s_wout8, 1)

            def contract(g, k):
                if first(g, 2):
                    pe.wait_ge(s_ys, 4 * g - 4)
                for f in range(FC):
                    for r, (part, ready) in enumerate(((hhi, s_hhi), (hlo, s_hlo))):
                        pe.wait_ge(ready, g * FC + f + 1)
                        for t in range(4):
                            bank = wide[2 * k + t // 2][:, (t % 2) * 512:(t % 2) * 512 + D]
                            mm = pe.matmul(bank, part[f % 4][:, t * P:(t + 1) * P], wout8[:, f, :],
                                           start=(f == 0 and r == 0), stop=(f == FC - 1 and r == 1))
                            if f == FC - 1 and r == 1:
                                mm.then_inc(s_acc, 1)
                            elif r == 1 and t == 3:
                                mm.then_inc(s_hused, 1)

            contract(0, 0)
            contract(1, 1)
            with pe.Fori(1, NG // 2) as j:
                for k in range(2):
                    contract(2 * j + k, k)

        @block.vector
        def _(dve):
            chain = [0]

            def link(ins):
                chain[0] += 1
                ins.then_inc(s_vc, 1)
                dve.wait_ge(s_vc, chain[0])

            def hold(u):
                if not isinstance(u, int):
                    dve.sem_inc(s_pace[0], 1)

            def stats(n, u, k):
                for t in range(2):
                    ins = dve.bn_stats(bn[n][k][:, t, :], xres[:, 2 * u + t, :])
                ins.then_inc(s_bn[n], 1)

            def aggregate(n, u, k):
                dve.wait_ge(s_bn[n], u + 1)
                hold(u)
                for t in range(2):
                    ins = dve.bn_aggr(mv[n][k][:, t, :], bn[n][k][:, t, :])
                ins.then_inc(s_mv[n], 1)

            def normalise(n, u, k, dst, done):
                dve.wait_ge(s_rstd[n], u + 1)
                hold(u)
                for t in range(2):
                    ins = dve.tensor_scalar(dst[k][:, t, :], xres[:, 2 * u + t, :], mv[n][k][:, t, 0:1],
                                            rstd[n][k][:, t:t + 1], ALU.subtract, ALU.mult)
                ins.then_inc(done, 1)

            def qk(u, k, t):
                n = 2 * u + t
                dve.wait_ge(s_q, u + 1)
                dve.wait_ge(s_kp, n + 1)
                dve.tensor_tensor(prod[t][:], ps_k[:].rearrange("p (o d) -> p o d", o=KW),
                                  q[k][:, t, :].unsqueeze(1).broadcast_to([P, KW, D]), ALU.mult).then_inc(s_prod, 1)

            def qk_sum(u, k, t):
                n = 2 * u + t
                dve.wait_ge(s_prod, n + 1)
                dve.tensor_reduce(s[k][:, t].rearrange("p o h -> p (o h)"),
                                  prod[t][:].rearrange("p o (h d) -> p (o h) d", h=H), AX.X, ALU.add).then_inc(s_red, 1)

            def softmax_shift(u, k):
                s3 = s[k][:].rearrange("p t o h -> p (t o) h")
                dve.wait_ge(s_red, 2 * u + 2)
                dve.tensor_tensor(s3, s3, neg[:, bass.ds(2 * u, 2), :].rearrange("p t o -> p (t o)").unsqueeze(2)
                                  .broadcast_to([P, 2 * KW, H]), ALU.add).then_inc(s_masked, 1)
                dve.wait_ge(s_masked, u + 1)
                dve.tensor_reduce(smax[k][:], s[k][:].rearrange("p t o h -> p t h o"), AX.X, ALU.max).then_inc(s_smax, 1)
                dve.wait_ge(s_smax, u + 1)
                dve.tensor_tensor(s[k][:], s[k][:], smax[k][:].unsqueeze(2).broadcast_to([P, 2, KW, H]),
                                  ALU.subtract).then_inc(s_shift, 1)

            def softmax_norm(u, k):
                if first(u, 2):
                    dve.wait_ge(s_pv, 2 * u - 2)
                dve.wait_ge(s_exp, u + 1)
                dve.tensor_reduce(ssum[k][:], e[k][:].rearrange("p t o h -> p t h o"), AX.X, ALU.add).then_inc(s_ssum, 1)
                dve.wait_ge(s_ssum, u + 1)
                dve.reciprocal(srec[k][:], ssum[k][:]).then_inc(s_srec, 1)
                dve.wait_ge(s_srec, u + 1)
                dve.tensor_tensor(pr[k][:], e[k][:], srec[k][:].unsqueeze(2).broadcast_to([P, 2, KW, H]),
                                  ALU.mult).then_inc(s_p, 1)

            def residual(u, k):
                xv = xres[:, bass.ds(2 * u, 2), :].rearrange("p t d -> p (t d)")
                dve.wait_ge(s_yp, u + 1)
                hold(u)
                dve.scalar_tensor_tensor(out=xv, in0=ps_y, scalar=tanhs[:, 0:1], in1=xv, op0=ALU.mult,
                                         op1=ALU.add).then_inc(s_x1, 1)

            def largest(u, k):
                dve.wait_ge(s_xn2, u + 1)
                hold(u)
                dve.tensor_reduce(xmax[:, bass.ds(u, 1)], xn2[k][:].rearrange("p t d -> p (t d)"), AX.X, ALU.max,
                                  apply_absolute_value=True).then_inc(s_xmax, 1)

            def step(i, k):
                on = lambda lag: not isinstance(i, int) or lag <= i < NP + lag
                if on(0):
                    stats(0, i, k)
                if on(1):
                    qk(i - 1, 1 - k, 0)
                if on(0):
                    aggregate(0, i, k)
                if on(1):
                    qk_sum(i - 1, 1 - k, 0)
                if on(3):
                    residual(i - 3, 1 - k)
                if on(1):
                    qk(i - 1, 1 - k, 1)
                if on(3):
                    dve.wait_ge(s_x1, i - 2)
                    hold(i)
                    stats(1, i - 3, 1 - k)
                if on(1):
                    qk_sum(i - 1, 1 - k, 1)
                if on(3):
                    aggregate(1, i - 3, 1 - k)
                if on(0):
                    if first(i, 2):
                        dve.wait_ge(s_xTp, i - 1)
                    normalise(0, i, k, xn, s_xn)
                if on(1):
                    softmax_shift(i - 1, 1 - k)
                if on(3):
                    if first(i, 5):
                        dve.wait_ge(s_xn2Tp, i - 4)
                    normalise(1, i - 3, 1 - k, xn2, s_xn2)
                    largest(i - 3, 1 - k)
                if on(1):
                    softmax_norm(i - 1, 1 - k)

            dve.wait_ge(s_x[0], 16)
            dve.wait_ge(s_wkvTp, 1)
            dve.tensor_copy(wkvT[:].rearrange("p c e -> p (c e)"), bank45[:]).then_inc(s_wkvT, 1)
            dve.wait_ge(s_segt, 16)
            link(dve.tensor_scalar(seg_f[:], seg_t[:], 0.0, None, ALU.max))
            for off in range(KW):
                ins = dve.tensor_scalar(neg[:, :, off], seg_f[:], float(off), NEG, ALU.is_lt, ALU.mult)
            ins.then_inc(s_neg, 1)
            dve.wait_ge(s_kv, NB)
            for b in range(0, NB, 2):
                ins = dve.tensor_reduce(kvp[:, 0, b:b + 2], wide[b // 2][0:U, :].rearrange("u (b n) -> u b n", b=2), AX.X, ALU.max,
                                        apply_absolute_value=True)
            link(ins)
            link(dve.tensor_scalar(kvp[:, 0, :], kvp[:, 0, :], 2.0 ** -96, None, ALU.max))
            link(dve.tensor_scalar(kvp[:, 1, :].bitcast(I32), kvp[:, 0, :].bitcast(I32), POW2_BITS, None, ALU.bitwise_and))
            link(dve.reciprocal(kvp[:, 2, :], kvp[:, 1, :]))
            dve.tensor_scalar(kvp[:, 3, :], kvp[:, 1, :], 1.0 / HALF_TOP, None, ALU.mult)
            link(dve.tensor_scalar(kvp[:, 2, :], kvp[:, 2, :], HALF_TOP, None, ALU.mult))
            dve.sem_inc(s_kvscale, 1)
            for b in range(NB):
                dve.wait_ge(s_kvhi, b + 1)
                t, c0 = kv_ap[b]
                dve.scalar_tensor_tensor(out=kvtab[:, b, 1, :], in0=t[0:U, c0:c0 + 2 * D], scalar=kvp[:, 2, b:b + 1],
                                         in1=kvtab[:, b, 0, :], op0=ALU.mult, op1=ALU.subtract).then_inc(s_kvlo, 1)
            step(0, 0)
            dve.wait_ge(s_jo, 1)
            for b in range(NB):
                dve.wait_ge(s_segc, b + 1)
                for off in range(KW):
                    ins = dve.tensor_scalar(onehot[:, off, b * LQ:(b + 1) * LQ], seg_b[:, b * LQ:(b + 1) * LQ],
                                            jo[:, off:off + 1], kvp[:, 3, b:b + 1], ALU.is_equal, ALU.mult)
                ins.then_inc(s_oh, 1)

            def row_scale(amax, sc):
                link(dve.tensor_scalar(amax[:], amax[:], AMAX_FLOOR, None, ALU.max))
                link(dve.reciprocal(sc[:], amax[:]))
                link(dve.tensor_scalar(sc[:], sc[:], W_LEVELS, None, ALU.mult))

            for hf in range(2):
                dve.wait_ge(s_winTp, hf + 1)
                ins = dve.tensor_reduce(amax_win[:, hf * 4:hf * 4 + 4], win_half[hf][:].rearrange("p (f d) -> p f d", f=FC // 2),
                                        AX.X, ALU.max, apply_absolute_value=True)
            link(ins)
            row_scale(amax_win, sc_win)
            for f in range(FC):
                ins = dve.tensor_scalar(w_i16[:, f, :], win_half[f // 4][:, (f % 4) * D:(f % 4 + 1) * D], sc_win[:, f:f + 1], None, ALU.mult)
            link(ins)
            dve.tensor_copy(win_f16[:], w_i16[:]).then_inc(s_winq, 1)
            dve.wait_ge(s_winq, 1)
            dve.wait_ge(s_wout, 16)
            link(dve.tensor_reduce(amax_wout[:], wout_ld[:], AX.X, ALU.max, apply_absolute_value=True))
            row_scale(amax_wout, sc_wout)
            for f in range(FC):
                ins = dve.tensor_scalar(w_i16[:, f, :], wout_ld[:, f, :], sc_wout[:, f:f + 1], None, ALU.mult)
            link(ins)
            dve.tensor_copy(wout8[:], w_i16[:]).then_inc(s_wout8, 1)
            dve.tensor_reduce(top_wout[:, 0:1], amax_wout[:], AX.X, ALU.max).then_inc(s_wrow, 1)
            dve.wait_ge(s_neg, 1)

            for i in range(1, 6):
                if i == 3:
                    dve.wait_ge(s_tanh, 1)
                if i == 4:
                    for b in range(1, NB):
                        dve.wait_ge(s_x[b], 16)
                step(i, i % 2)
            with dve.Fori(3, NP // 2) as j:
                for k in range(2):
                    step(2 * j + k, k)
            for i in range(NP, NP + 4):
                step(i, i % 2)

            dve.wait_ge(s_xmax, NP)
            dve.tensor_reduce(qx[:, 0:1], xmax[:], AX.X, ALU.max).then_inc(s_xall, 1)
            dve.wait_ge(s_wall, 1)
            link(dve.reciprocal(top_wout[:, 2:3], top_wout[:, 1:2]))
            link(dve.tensor_scalar(rel_wout[:], amax_wout[:], top_wout[:, 2:3], None, ALU.mult))
            dve.tensor_scalar(bout[:], bout[:], tanhs[:, 1:2], None, ALU.mult).then_inc(s_bias, 1)
            dve.wait_ge(s_qxr, 1)
            link(dve.tensor_scalar(qx[:, 2:3], qx[:, 1:2], AMAX_FLOOR, None, ALU.max))
            link(dve.reciprocal(qx[:, 3:4], qx[:, 2:3]))
            link(dve.tensor_scalar(qx[:, 3:4], qx[:, 3:4], A_LEVELS, None, ALU.mult))
            link(dve.tensor_scalar(qx[:, 4:5], qx[:, 2:3], 1.0 / (A_LEVELS * W_LEVELS), None, ALU.mult))
            dve.tensor_scalar(zscale[:], amax_win[:], qx[:, 4:5], None, ALU.mult).then_inc(s_qxs, 1)

            def quantise_x(g, k):
                n = 2 if isinstance(g, int) and g < 2 else 0
                if not n:
                    dve.wait_ge(s_z, (g - 1) * FC)
                    hold(g)
                dve.tensor_scalar(xr[k][:], xn2T[:, g, :, :], qx[:, 3:4], None, ALU.mult).then_inc(s_xr, 1)
                dve.wait_ge(s_xr, g + 1)
                dve.tensor_copy(xhi[k][:], xr[k][:]).then_inc(s_xhi, 1)
                dve.wait_ge(s_xhi, g + 1)
                dve.tensor_tensor(xlo[k][:], xr[k][:], xhi[k][:], ALU.subtract).then_inc(s_xq, 1)

            def hidden_max(g, m):
                dve.wait_ge(s_h, g * FC + 2 * m + 2)
                hold(g)
                dve.tensor_reduce(hmax[:, bass.ds(g * (FC // 2) + m, 1)], hidden[:, g, 2 * m:2 * m + 2, :], AX.XY, ALU.max,
                                  apply_absolute_value=True).then_inc(s_hm, 1)

            def stage_b(g, k, last=False):
                hidden_max(g, 0)
                hidden_max(g, 1)
                if not last:
                    quantise_x(g + 1, 1 - k)
                hidden_max(g, 2)
                hidden_max(g, 3)

            quantise_x(0, 0)
            stage_b(0, 0)
            stage_b(1, 1)
            with dve.Fori(1, NG // 2 - 1) as j:
                for k in range(2):
                    stage_b(2 * j + k, k)
            stage_b(NG - 2, 0)
            stage_b(NG - 1, 1, last=True)

            dve.wait_ge(s_hm, NG * FC // 2)
            dve.tensor_reduce(qh[:, 0:1], hmax[:], AX.X, ALU.max).then_inc(s_hall, 1)
            dve.wait_ge(s_qhr, 1)
            link(dve.tensor_scalar(qh[:, 2:3], qh[:, 1:2], AMAX_FLOOR, None, ALU.max))
            link(dve.reciprocal(qh[:, 3:4], qh[:, 2:3]))
            link(dve.tensor_scalar(qh[:, 3:4], qh[:, 3:4], A_LEVELS, None, ALU.mult))
            link(dve.tensor_scalar(qh[:, 4:5], qh[:, 2:3], 1.0 / (A_LEVELS * W_LEVELS), None, ALU.mult))
            link(dve.tensor_scalar(qh[:, 4:5], qh[:, 4:5], top_wout[:, 1:2], None, ALU.mult))
            dve.tensor_scalar(qh[:, 5:6], qh[:, 4:5], tanhs[:, 1:2], None, ALU.mult).then_inc(s_qhs, 1)

            def split_h(g, f):
                src = hq[f // 2 % 2][:, f % 2, :]
                if f % 2 == 0:
                    dve.wait_ge(s_hq, g * (FC // 2) + f // 2 + 1)
                if f >= 4:
                    dve.wait_ge(s_hused, g * (FC - 1) + f - 3)
                elif not isinstance(g, int) or g:
                    if f < 3:
                        dve.wait_ge(s_hused, g * (FC - 1) + f - 2)
                    else:
                        dve.wait_ge(s_acc, g * 4)
                dve.tensor_scalar(hhi[f % 4][:], src, rel_wout[:, f:f + 1], None, ALU.mult).then_inc(s_hhi, 1)
                dve.wait_ge(s_hhi, g * FC + f + 1)
                dve.scalar_tensor_tensor(out=hlo[f % 4][:], in0=src, scalar=rel_wout[:, f:f + 1], in1=hhi[f % 4][:],
                                         op0=ALU.mult, op1=ALU.subtract).then_inc(s_hlo, 1)

            for f in range(FC):
                split_h(0, f)
            with dve.Fori(1, NG) as g:
                for f in range(FC):
                    split_h(g, f)


_INS = ["x", "ctx_1024", "itok_BxS_0_511", "g_xattn", "g_ffn", "L0_xattn_Wq", "L0_xattn_Wkv", "L0_xattn_Wo",
        "L0_ffn_W_in", "L0_ffn_b_in", "L0_ffn_W_out", "L0_ffn_b_out"]


def kernel(**inputs):
    import numpy as _np
    import concourse.bacc as _bacc
    from concourse import mybir as _mybir
    from concourse.bass_utils import run_bass_kernel_spmd as _run

    nc = _bacc.Bacc("TRN2", target_bir_lowering=False, num_devices=1)
    arrays, args = {}, []
    for name in _INS:
        a = _np.ascontiguousarray(inputs[name])
        arrays[f"in_{name}_dram"] = a
        args.append(nc.dram_tensor(f"in_{name}_dram", a.shape, _mybir.dt.from_np(a.dtype), kind="ExternalInput").ap())
    out = nc.dram_tensor("out_dram", arrays["in_x_dram"].shape, _mybir.dt.float32, kind="ExternalOutput").ap()
    flamingo_kernel(nc, *args, out)
    r = _run(nc, [arrays], core_ids=[0])
    return r.results[0]["out_dram"]
```

```python
from contextlib import ExitStack

import concourse.bass as bass
from concourse import mybir

P = 128
ALU = mybir.AluOpType
ACT = mybir.ActivationFunctionType
AX = mybir.AxisListType
F32 = mybir.dt.float32
F16 = mybir.dt.float16
BF16 = mybir.dt.bfloat16
I16 = mybir.dt.int16
I32 = mybir.dt.int32
RMAX = bass.bass_isa.ReduceOp.max

LN_EPS = 1e-5
AMAX_FLOOR = 1e-8
W_LEVELS = 127.0
A_LEVELS = 32767.0
NEG = -3.4028234663852886e38
POW2_BITS = 0x7F800000
HALF_TOP = 16384.0


def flamingo_kernel(nc, x, ctx_kv, seg, g_xattn, g_ffn, w_q, w_kv, w_o, w_in, b_in, w_out, b_out, out):
    NB, LQ, D = x.shape
    LKV = ctx_kv.shape[1]
    F = w_in.shape[1]
    H, HD = 16, D // 16
    KW = 4
    U = LKV + KW - 1
    C = D // P
    FC = F // P
    TB = LQ // P
    NT = NB * TB
    NP = NT // 2
    NG = NT // 4
    GT = 4 * P
    SCALE = float(HD) ** -0.5

    with ExitStack() as ctx:
        def sem(name):
            return ctx.enter_context(nc.semaphore(name))

        base = (nc.sbuf_base + 63) // 64 * 64
        size = {F32: 4, I32: 4, F16: 2, BF16: 2, I16: 2}

        class Region:
            def __init__(self, start, length):
                self.at, self.end = start, start + length

            def put(self, name, shape, dt):
                n = size[dt]
                for d in shape[1:]:
                    n *= d
                off = (self.at + 31) // 32 * 32
                self.at = off + n
                assert self.at <= self.end, (name, self.at - self.end)
                return nc.alloc_sbuf_tensor_at(name, shape, dt, offset=off)

        HID = FC * GT * 4 * NG
        SLOT = HID // NG
        XN2T = C * NT * P * 4
        RES = NT * D * 4
        hid_r = Region(base, HID)
        a_r = Region(base, HID - XN2T)
        x2_r = Region(base + HID - XN2T, XN2T)
        pre_r = Region(base + HID - XN2T, XN2T)
        keep_r = Region(base + HID, RES + 12800)
        bc_r = Region(base + HID + RES + 12800, nc.sbuf_usable_end - (base + HID + RES + 12800))
        pre2_r = Region(base + HID + RES + 12800, nc.sbuf_usable_end - (base + HID + RES + 12800))

        hidden = hid_r.put("hidden", [P, NG, FC, GT], F32)
        xn2T = x2_r.put("xn2T", [P, NG, C, GT], F32)

        xres = keep_r.put("xres", [P, NT, D], F32)
        win8 = keep_r.put("win8", [P, C, F], F16)
        wout8 = keep_r.put("wout8", [P, FC, D], F16)
        ident = keep_r.put("ident", [P, P], F32)
        ident16 = keep_r.put("ident16", [P, P], F16)
        neg = keep_r.put("neg", [P, NT, KW], F32)
        bout = keep_r.put("bout", [P, D], F32)
        bin_ = keep_r.put("bin_", [P, FC], F32)
        bin_ld = keep_r.put("bin_ld", [FC, P], F32)
        gates = keep_r.put("gates", [P, 2], F32)
        tanhs = keep_r.put("tanhs", [P, 2], F32)
        amax_win = keep_r.put("amax_win", [P, FC], F32)
        amax_wout = keep_r.put("amax_wout", [P, FC], F32)
        sc_win = keep_r.put("sc_win", [P, FC], F32)
        sc_wout = keep_r.put("sc_wout", [P, FC], F32)
        rel_wout = keep_r.put("rel_wout", [P, FC], F32)
        top_wout = keep_r.put("top_wout", [P, 3], F32)
        zscale = keep_r.put("zscale", [P, FC], F32)
        qx = keep_r.put("qx", [P, 8], F32)
        qh = keep_r.put("qh", [P, 8], F32)
        hmax = keep_r.put("hmax", [P, NG * FC // 2], F32)
        xmax = keep_r.put("xmax", [P, NP], F32)
        consts = keep_r.put("consts", [P, 8], F32)

        onehot = a_r.put("onehot", [U, KW, NT * P], BF16)
        kvtab = a_r.put("kvtab", [U, NB, 2, 2 * D], F16)
        wqT = a_r.put("wqT", [P, C, D], F32)
        woT = a_r.put("woT", [P, C, D], F32)

        def pair(name, shape, dt=F32):
            return [a_r.put(f"{name}{i}", shape, dt) for i in range(2)]

        xn, xT, q = pair("xn", [P, 2, D]), pair("xT", [P, C, 2 * P]), pair("q", [P, 2, D])
        prod, vsel = pair("prod", [P, KW, D]), pair("vsel", [P, KW, D])
        o, oT, xn2 = pair("o", [P, 2, D]), pair("oT", [P, C, 2 * P]), pair("xn2", [P, 2, D])
        s, e, pr = pair("s", [P, 2, KW, H]), pair("e", [P, 2, KW, H]), pair("pr", [P, 2, KW, H])
        smax, ssum, srec = pair("smax", [P, 2, H]), pair("ssum", [P, 2, H]), pair("srec", [P, 2, H])
        bn = [pair("bn1_", [P, 2, 6]), pair("bn2_", [P, 2, 6])]
        mv, ve, rstd, nbias = pair("mv", [P, 4, 2]), pair("ve", [P, 4]), pair("rstd", [P, 4]), pair("nbias", [P, 4])
        ctxT = a_r.put("ctxT", [P, C, NB * U], F32)
        wkvT = pre2_r.put("wkvT", [P, C, 2 * D], F32)

        seg_i = pre_r.put("seg_i", [U, NB * LQ], I32)
        seg_b = pre_r.put("seg_b", [U, NB * LQ], BF16)
        wkv_ld = pre_r.put("wkv_ld", [P, 2 * C, D], F32)
        ctx_ld = pre_r.put("ctx_ld", [U, NB, D], F32)
        wq_ld = pre2_r.put("wq_ld", [P, C, D], F32)
        wo_ld = pre2_r.put("wo_ld", [P, C, D], F32)
        win_ld = pre2_r.put("win_ld", [P, C, F], F32)
        wout_ld = pre2_r.put("wout_ld", [P, FC, D], F32)
        w_i16 = pre2_r.put("w_i16", [P, FC, D], I16)
        win_f16 = pre2_r.put("win_f16", [P, FC, D], F16)
        seg_t = keep_r.put("seg_t", [P, NT], I32)
        seg_f = keep_r.put("seg_f", [P, NT], F32)
        jo = keep_r.put("jo", [U, KW], F32)
        kvp = keep_r.put("kvp", [U, 4, NB], F32)

        xr = [bc_r.put(f"xr{i}", [P, C, GT], I16) for i in range(2)]
        xhi = [bc_r.put(f"xhi{i}", [P, C, GT], F16) for i in range(2)]
        xlo = [bc_r.put(f"xlo{i}", [P, C, GT], F16) for i in range(2)]
        c_r = Region(base + HID + RES + 12800, nc.sbuf_usable_end - (base + HID + RES + 12800))
        hq = [c_r.put(f"hq{i}", [P, 2, GT], I16) for i in range(FC // 2)]
        hhi = [c_r.put(f"hhi{i}", [P, GT], F16) for i in range(FC)]
        hlo = [c_r.put(f"hlo{i}", [P, GT], F16) for i in range(FC)]
        y = [c_r.put(f"y{i}", [P, 4, D], F32) for i in range(2)]

        bank01 = ctx.enter_context(nc.psum_tensor("bank01", [P, 1024], F32))
        bank23 = ctx.enter_context(nc.psum_tensor("bank23", [P, 1024], F32))
        bank45 = ctx.enter_context(nc.psum_tensor("bank45", [P, 1024], F32))
        bank67 = ctx.enter_context(nc.psum_tensor("bank67", [P, 1024], F32))
        wide = [bank01, bank23, bank45, bank67]
        ps_k, ps_v = bank01, bank23
        ps_t, ps_q = bank45[:, 0:512], bank45[:, 512:1024]
        ps_o, ps_y = bank67[:, 0:512], bank67[:, 512:1024]

        s_x = [sem(f"x_loaded{b}") for b in range(NB)]
        s_ctx, s_wkv, s_segb, s_segt = sem("ctx_loaded"), sem("wkv_loaded"), [sem(f"segb_loaded{b}") for b in range(NB)], sem("segt_loaded")
        s_wq, s_wo, s_win, s_wout = sem("wq_loaded"), sem("wo_loaded"), sem("win_loaded"), sem("wout_loaded")
        s_small, s_gate = sem("bin_loaded"), sem("gates_bout_loaded")
        s_ident0, s_ident, s_jo = sem("ident_zeroed"), sem("ident_ready"), sem("jo_ready")
        s_const = sem("consts_ready")
        s_winsc = sem("win_scales_ready")
        s_hhia = sem("hidden_hi_ready_scalar")
        s_ctxTp, s_ctxT, s_wkvTp, s_wkvT = sem("ctxT_in_psum"), sem("ctxT_ready"), sem("wkvT_in_psum"), sem("wkvT_ready")
        s_wqTp, s_wqT, s_woTp, s_woT = sem("wqT_in_psum"), sem("wqT_ready"), sem("woT_in_psum"), sem("woT_ready")
        s_kv, s_kvscale, s_kvhi, s_kvlo = sem("kv_in_psum"), sem("kv_scales"), sem("kv_hi_ready"), sem("kv_lo_ready")
        s_oh, s_neg = sem("onehot_ready"), sem("neg_ready")
        s_winTp, s_winq, s_w8p, s_w8 = sem("winT_in_psum"), sem("win_quantised"), sem("win8_in_psum"), sem("win8_ready")
        s_wout8, s_rel = sem("wout8_ready"), sem("wout_row_ratio")
        s_tanh = sem("tanh_ready")
        s_vc = sem("vector_setup_chain")
        s_bn = [sem("stats1_parts"), sem("stats2_parts")]
        s_mv, s_ve, s_rstd, s_nb = sem("mean_var_ready"), sem("var_eps_ready"), sem("rstd_ready"), sem("norm_bias_ready")
        s_xn, s_xTp, s_xT = sem("xn_ready"), sem("xT_in_psum"), sem("xT_ready")
        s_qp, s_q = sem("q_in_psum"), sem("q_ready")
        s_kp, s_prod, s_red = sem("k_in_psum"), sem("qk_products"), sem("scores_summed")
        s_masked, s_smax, s_shift = sem("scores_masked"), sem("score_max"), sem("scores_shifted")
        s_exp, s_ssum, s_srec, s_p = sem("exp_ready"), sem("exp_sum"), sem("exp_sum_inv"), sem("probs_ready")
        s_vp, s_vc2 = sem("v_in_psum"), sem("v_copied")
        s_pv, s_pv2, s_o = sem("pv_products"), sem("pv_halves"), sem("o_tile_ready")
        s_oTp, s_oT, s_yp, s_x1 = sem("oT_in_psum"), sem("oT_ready"), sem("attn_out_in_psum"), sem("x1_ready")
        s_xn2, s_xn2Tp, s_xn2T = sem("xn2_ready"), sem("xn2T_in_psum"), sem("xn2T_ready")
        s_xmax = sem("xn2_max")
        s_pace = [sem("pace_vector"), sem("pace_scalar")]
        s_xall, s_qxr, s_qxs = sem("x_amax_row"), sem("x_amax_all"), sem("x_scale_ready")
        s_bias = sem("bout_scaled")
        s_xr, s_xhi, s_xq = sem("x_rounded"), sem("x_hi_ready"), sem("x_quantised")
        s_z, s_h, s_hm = sem("z_in_psum"), sem("hidden_ready"), sem("hidden_pair_max")
        s_hall, s_qhr, s_qhs = sem("h_amax_row"), sem("h_amax_all"), sem("h_scale_ready")
        s_wrow, s_wall = sem("wout_amax_row"), sem("wout_amax_all")
        s_x1b = sem("x1_with_bias")
        s_hq, s_hhi, s_hlo = sem("hidden_rounded"), sem("hidden_hi_ready"), sem("hidden_lo_ready")
        s_hused, s_acc, s_ys, s_out = sem("hidden_chunk_used"), sem("out_in_psum"), sem("out_scaled"), sem("out_ready")
        s_stored = [sem("stored_even"), sem("stored_odd")]

        x_d = x.rearrange("b (p t) d -> b p t d", p=P)
        out_d = out.rearrange("b (p t) d -> b p t d", p=P)
        kv_ap = [(bank23, b % 2 * 512) for b in range(NB)]
        ON_ACT = (3, FC - 1)

        BIN_AT = NB * U

        def by_dve(f):
            return f - sum(a < f for a in ON_ACT)

        def first(u, n):
            return not isinstance(u, int) or u >= n

        block = ctx.enter_context(nc.Block())

        @block.sync
        def _(sp):
            sp.dma_start(ctx_ld[0:LKV, :, :], ctx_kv.rearrange("b j d -> j b d")).then_inc(s_ctx, 16)
            sp.dma_start(wkv_ld[:], w_kv.rearrange("(c p) d -> p c d", p=P)).then_inc(s_wkv, 16)
            sp.dma_start(xres[:, 0:TB, :], x_d[0]).then_inc(s_x[0], 16)
            sp.dma_start(wo_ld[:], w_o.rearrange("(c p) d -> p c d", p=P)).then_inc(s_wo, 16)
            sp.dma_start(win_ld[:], w_in.rearrange("(c p) f -> p c f", p=P)).then_inc(s_win, 16)
            for b in range(1, NB):
                sp.dma_start(seg_i[:, b * LQ:(b + 1) * LQ], seg[b].partition_broadcast(U)).then_inc(s_segb[b], 16)
            for b in range(1, NB):
                sp.dma_start(xres[:, TB * b:TB * (b + 1), :], x_d[b]).then_inc(s_x[b], 16)
            sp.dma_start(wout_ld[:], w_out.rearrange("(c p) d -> p c d", p=P)).then_inc(s_wout, 16)
            for g in range(NG):
                b, t0 = g * 4 // TB, g * 4 % TB
                sp.wait_ge(s_out, g + 1)
                sp.dma_start(out_d[b, :, t0:t0 + 4, :], y[g % 2][:]).then_inc(s_stored[g % 2], 16)
            for k in range(2):
                sp.wait_ge(s_stored[k], 16 * (NG // 2))

        @block.gpsimd
        def _(pool):
            pool.memset(ident[:], 0.0).then_inc(s_ident0, 1)
            pool.memset(ident16[:], 0.0).then_inc(s_ident0, 1)
            pool.memset(consts[:, 0:4], LN_EPS).then_inc(s_const, 1)
            pool.memset(consts[:, 4:8], -0.5).then_inc(s_const, 1)
            pool.wait_ge(s_ident0, 2)
            for m in (ident, ident16):
                pool.affine_select(out=m[:], in_=m[:], compare_op=ALU.not_equal, fill=1.0, base=0,
                                   pattern=[[-1, P]], channel_multiplier=1).then_inc(s_ident, 1)
            pool.iota(jo[:], pattern=[[1, KW]], base=0, channel_multiplier=1,
                      allow_small_or_imprecise_dtypes=True).then_inc(s_jo, 1)

            def inv_std(i, k):
                at = slice(0 if not isinstance(i, int) or i < NP else 2, 4 if not isinstance(i, int) or i >= 4 else 2)
                w = at.stop - at.start
                pool.wait_ge(s_mv, i + 1)
                pool.tensor_tensor(ve[k][:, at], mv[k][:, at, 1], consts[:, 0:w], ALU.add).then_inc(s_ve, 1)
                pool.wait_ge(s_ve, i + 1)
                pool.tensor_tensor(rstd[k][:, at], ve[k][:, at], consts[:, 4:4 + w], ALU.pow).then_inc(s_rstd, 1)

            def weigh_v(u, k, t):
                n = 2 * u + t
                v3 = vsel[t][:].rearrange("p o (h d) -> p (o h) d", h=H)
                pool.wait_ge(s_vc2, n + 1)
                pool.wait_ge(s_p, u + 1)
                pool.tensor_tensor(v3, v3, pr[k][:, t].rearrange("p o h -> p (o h)").unsqueeze(2).broadcast_to([P, KW * H, HD]),
                                   ALU.mult).then_inc(s_pv, 1)
                pool.wait_ge(s_pv, n + 1)
                pool.tensor_tensor(vsel[t][:, 0:2, :], vsel[t][:, 0:2, :], vsel[t][:, 2:4, :], ALU.add).then_inc(s_pv2, 1)
                pool.wait_ge(s_pv2, n + 1)
                if first(u, 2):
                    pool.wait_ge(s_oTp, u - 1)
                pool.tensor_tensor(o[k][:, t, :], vsel[t][:, 0, :], vsel[t][:, 1, :], ALU.add).then_inc(s_o, 1)

            def step(i, k):
                if not isinstance(i, int) or i < NP + 4:
                    inv_std(i, k)
                if not isinstance(i, int) or 2 <= i < NP + 2:
                    weigh_v(i - 2, k, 0)
                    weigh_v(i - 2, k, 1)

            pool.wait_ge(s_const, 2)
            for i in range(6):
                step(i, i % 2)
            with pool.Fori(3, NP // 2) as j:
                for k in range(2):
                    step(2 * j + k, k)
            for i in range(NP, NP + 5):
                step(i, i % 2)

            pool.wait_ge(s_xall, 1)
            pool.partition_all_reduce(qx[:, 1:2], qx[:, 0:1], P, RMAX).then_inc(s_qxr, 1)
            pool.wait_ge(s_wrow, 1)
            pool.partition_all_reduce(top_wout[:, 1:2], top_wout[:, 0:1], P, RMAX).then_inc(s_wall, 1)
            pool.wait_ge(s_bias, 1)
            for g in range(NG):
                v = xres[:, 4 * g:4 * g + 4, :]
                pool.tensor_tensor(v, v, bout[:].unsqueeze(1).broadcast_to([P, 4, D]), ALU.add).then_inc(s_x1b, 1)
            pool.wait_ge(s_hall, 1)
            pool.partition_all_reduce(qh[:, 1:2], qh[:, 0:1], P, RMAX).then_inc(s_qhr, 1)
            pool.wait_ge(s_x1b, NG)

            def add_residual(g, k):
                pool.wait_ge(s_ys, 4 * g + 4)
                pool.tensor_tensor(y[k][:], y[k][:], xres[:, bass.ds(4 * g, 4), :], ALU.add).then_inc(s_out, 1)

            with pool.Fori(0, NG // 2) as j:
                for k in range(2):
                    add_residual(2 * j + k, k)

        @block.scalar
        def _(act):
            act.dma_start(ctx_ld[LKV:U, :, :], ctx_kv[:, LKV - 1, :].partition_broadcast(U - LKV)).then_inc(s_ctx, 16)
            act.dma_start(bin_ld[:], b_in.rearrange("(c p) -> c p", p=P)).then_inc(s_small, 16)
            act.dma_start(wq_ld[:], w_q.rearrange("(c p) d -> p c d", p=P)).then_inc(s_wq, 16)
            act.dma_start(seg_i[:, 0:LQ], seg[0].partition_broadcast(U)).then_inc(s_segb[0], 16)
            act.dma_start(seg_t[:].rearrange("p (b t) -> p b t", b=NB), seg.rearrange("b (p t) -> p b t", p=P)).then_inc(s_segt, 16)
            act.dma_start(gates[:, 0:1], g_xattn.partition_broadcast(P)).then_inc(s_gate, 16)
            act.dma_start(gates[:, 1:2], g_ffn.partition_broadcast(P)).then_inc(s_gate, 16)
            act.dma_start(bout[:], b_out.partition_broadcast(P)).then_inc(s_gate, 16)

            def copy(dst, src):
                return act.activation(dst, src, ACT.Copy)

            def hold(i):
                if not isinstance(i, int):
                    act.sem_inc(s_pace[1], 1)

            act.wait_ge(s_ctxTp, 1)
            copy(ctxT[:], bank67[:].rearrange("p (c n) -> p c n", c=C)[:, :, 0:NB * U]).then_inc(s_ctxT, 1)
            copy(bin_[:], bank67[:, BIN_AT:BIN_AT + FC]).then_inc(s_ctxT, 1)
            act.wait_ge(s_wqTp, 1)
            copy(wqT[:].rearrange("p c d -> p (c d)"), ps_o).then_inc(s_wqT, 1)

            def kv_high(b):
                act.wait_ge(s_kvscale, b // 2 + 1)
                t, c0 = kv_ap[b]
                act.activation(kvtab[:, b, 0, :], t[0:U, c0:c0 + 2 * D], ACT.Copy, scale=kvp[:, 2, b:b + 1]).then_inc(s_kvhi, 1)

            def round_win(hf):
                act.wait_ge(s_winsc, hf + 1)
                for f in range(hf * FC // 2, (hf + 1) * FC // 2):
                    at = f % (FC // 2) * D
                    ins = act.activation(w_i16[:, f, :], bank67[:, at:at + D], ACT.Copy, scale=sc_win[:, f:f + 1])
                ins.then_inc(s_winq, 1)
                act.wait_ge(s_winq, 2 * hf + 1)
                fs = slice(hf * FC // 2, (hf + 1) * FC // 2)
                copy(win_f16[:, fs, :], w_i16[:, fs, :]).then_inc(s_winq, 1)

            def norm1(i, k):
                if first(i, 2):
                    act.wait_ge(s_xTp, i - 1)
                act.wait_ge(s_nb, i + 1)
                hold(i)
                for t in range(2):
                    ins = act.activation(xn[k][:, t, :], xres[:, 2 * i + t, :], ACT.Identity,
                                         bias=nbias[k][:, t:t + 1], scale=rstd[k][:, t:t + 1])
                ins.then_inc(s_xn, 1)

            def norm2(i, u, k):
                if first(u, 2):
                    act.wait_ge(s_xn2Tp, u - 1)
                    act.wait_ge(s_xmax, u - 1)
                act.wait_ge(s_nb, i + 1)
                hold(i)
                for t in range(2):
                    ins = act.activation(xn2[k][:, t, :], xres[:, 2 * u + t, :], ACT.Identity,
                                         bias=nbias[k][:, 2 + t:3 + t], scale=rstd[k][:, 2 + t:3 + t])
                ins.then_inc(s_xn2, 1)

            def evac_oT(u, k):
                act.wait_ge(s_oTp, u + 1)
                if first(u, 2):
                    act.wait_ge(s_yp, u - 1)
                copy(oT[k][:].rearrange("p c n -> p (c n)"), ps_o).then_inc(s_oT, 1)

            def copy_v(u, t):
                n = 2 * u + t
                act.wait_ge(s_vp, n + 1)
                if first(n, 2):
                    act.wait_ge(s_o, n - 1)
                copy(vsel[t][:].rearrange("p o d -> p (o d)"), ps_v[:]).then_inc(s_vc2, 1)

            def exp(u, k):
                act.wait_ge(s_shift, u + 1)
                act.activation(e[k][:].rearrange("p t o h -> p (t o h)"), s[k][:].rearrange("p t o h -> p (t o h)"),
                               ACT.Exp, scale=SCALE).then_inc(s_exp, 1)

            def evac_xn2T(u, k):
                act.wait_ge(s_xn2Tp, u + 1)
                hold(u)
                copy(xn2T[:, u // 2, :, k * 2 * P:(k + 1) * 2 * P], ps_t.rearrange("p (c n) -> p c n", c=C)).then_inc(s_xn2T, 1)

            def evac_xT(u, k):
                act.wait_ge(s_xTp, u + 1)
                if first(u, 2):
                    act.wait_ge(s_qp, u - 1)
                copy(xT[k][:].rearrange("p c n -> p (c n)"), ps_t).then_inc(s_xT, 1)

            def evac_q(u, k):
                act.wait_ge(s_qp, u + 1)
                if first(u, 2):
                    act.wait_ge(s_prod, 2 * u - 2)
                copy(q[k][:].rearrange("p t d -> p (t d)"), ps_q).then_inc(s_q, 1)

            def step(i, k, before_xT=None):
                on = lambda lag: not isinstance(i, int) or lag <= i < NP + lag
                if on(2):
                    exp(i - 2, k)
                    copy_v(i - 2, 0)
                if on(5):
                    evac_xn2T(i - 5, 1 - k)
                if on(3):
                    evac_oT(i - 3, 1 - k)
                if on(2):
                    copy_v(i - 2, 1)
                if on(0):
                    norm1(i, k)
                if before_xT:
                    before_xT()
                if on(0):
                    evac_xT(i, k)
                if on(4):
                    norm2(i, i - 4, k)
                if on(0):
                    evac_q(i, k)

            norm1(0, 0)
            evac_xT(0, 0)
            act.wait_ge(s_woTp, 1)
            copy(woT[:].rearrange("p c d -> p (c d)"), ps_y).then_inc(s_woT, 1)
            kv_high(0)
            kv_high(1)
            evac_q(0, 0)
            act.wait_ge(s_gate, 48)
            act.activation(tanhs[:], gates[:], ACT.Tanh).then_inc(s_tanh, 1)
            round_win(0)
            kv_high(2)
            kv_high(3)
            step(1, 1)
            round_win(1)

            def keep_win8():
                act.wait_ge(s_w8p, 1)
                copy(win8[:].rearrange("p c f -> p (c f)"), bank67[:].bitcast(F16)).then_inc(s_w8, 1)

            step(2, 0, before_xT=keep_win8)
            for i in range(3, 6):
                step(i, i % 2)
            with act.Fori(3, NP // 2) as j:
                for k in range(2):
                    step(2 * j + k, k)
            for i in range(NP, NP + 5):
                step(i, i % 2)

            act.wait_ge(s_qxs, 1)
            act.activation(qx[:, 6:7], consts[:, 0:1], ACT.Gelu)
            def gelu(g, k):
                for f in range(FC):
                    act.wait_ge(s_z, g * FC + f + 1)
                    hold(g)
                    bank = wide[f // 2 % 4][:, (f % 2) * 512:(f % 2) * 512 + GT]
                    act.activation(hidden[:, g, f, :], bank, ACT.Gelu, bias=bin_[:, f:f + 1],
                                   scale=zscale[:, f:f + 1]).then_inc(s_h, 1)

            with act.Fori(0, NG) as g:
                gelu(g, 0)

            act.wait_ge(s_qhs, 2)

            def round_h(g, k):
                for m in range(FC // 2):
                    n = g * (FC // 2) + m
                    if first(n, FC // 2):
                        act.wait_ge(s_hlo, 2 * n + 2 - FC)
                        hold(g)
                    act.activation(hq[m][:], hidden[:, g, 2 * m:2 * m + 2, :], ACT.Copy,
                                   scale=qh[:, 3:4]).then_inc(s_hq, 1)
                    f = 2 * m + 1
                    if f in ON_ACT:
                        act.wait_ge(s_hq, n + 1)
                        if first(g, 1):
                            if f == FC - 1:
                                act.wait_ge(s_acc, g * 4)
                            else:
                                act.wait_ge(s_hused, (g - 1) * (FC - 1) + f + 1)
                        act.activation(hhi[f][:], hq[m][:, 1, :], ACT.Copy,
                                       scale=rel_wout[:, f:f + 1]).then_inc(s_hhia, 1)

            def scale_out(g, k):
                if first(g, 2):
                    act.wait_ge(s_stored[k], 8 * g - 8 * k)
                for t in range(4):
                    act.wait_ge(s_acc, g * 4 + t + 1)
                    bank = wide[2 * k + t // 2][:, (t % 2) * 512:(t % 2) * 512 + D]
                    act.activation(y[k][:, t, :], bank, ACT.Copy, scale=qh[:, 5:6]).then_inc(s_ys, 1)

            round_h(0, 0)
            for g in range(1, 4):
                round_h(g, g % 2)
                scale_out(g - 1, 1 - g % 2)
            with act.Fori(2, NG // 2) as j:
                for k in range(2):
                    round_h(2 * j + k, k)
                    scale_out(2 * j + k - 1, 1 - k)
            scale_out(NG - 1, 1)

        @block.tensor
        def _(pe):
            pe.wait_ge(s_ident, 2)
            pe.wait_ge(s_ctx, 32)
            for b in range(NB):
                for c in range(C):
                    mm = pe.transpose(bank67[:, c * 512 + b * U:c * 512 + (b + 1) * U], ctx_ld[:, b, c * P:(c + 1) * P],
                                      ident[0:U, 0:U])
            pe.wait_ge(s_small, 16)
            mm = pe.transpose(bank67[:, BIN_AT:BIN_AT + FC], bin_ld[:], ident[0:FC, 0:FC])
            mm.then_inc(s_ctxTp, 1)
            pe.wait_ge(s_wkv, 16)
            for r in range(2 * C):
                for c in range(C):
                    mm = pe.transpose(bank45[:, c * 512 + r * P:c * 512 + (r + 1) * P], wkv_ld[:, r, c * P:(c + 1) * P], ident[:])
            mm.then_inc(s_wkvTp, 1)

            def weight_T(dst, ld, landed, done):
                pe.wait_ge(landed, 16)
                for r in range(C):
                    for c in range(C):
                        mm = pe.transpose(dst[:, c * D + r * P:c * D + (r + 1) * P], ld[:, r, c * P:(c + 1) * P], ident[:])
                mm.then_inc(done, 1)

            pe.wait_ge(s_ctxT, 2)
            weight_T(ps_o, wq_ld, s_wq, s_wqTp)
            pe.wait_ge(s_wkvT, 1)

            def project_kv(b):
                t, c0 = kv_ap[b]
                for c in range(C):
                    mm = pe.matmul(t[0:U, c0:c0 + 2 * D], ctxT[:, c, b * U:(b + 1) * U], wkvT[:, c, :],
                                   start=(c == 0), stop=(c == C - 1))
                mm.then_inc(s_kv, 1)

            project_kv(0)
            project_kv(1)

            def transpose_o(u, k):
                pe.wait_ge(s_o, 2 * u + 2)
                if first(u, 1):
                    pe.wait_ge(s_oT, u)
                for t in range(2):
                    for c in range(C):
                        mm = pe.transpose(ps_o[:, c * 2 * P + t * P:c * 2 * P + (t + 1) * P], o[k][:, t, c * P:(c + 1) * P], ident[:])
                mm.then_inc(s_oTp, 1)

            def gather(dst, col, u, t, done):
                tile = 2 * u + t
                b = u // (TB // 2)
                for off in range(KW):
                    for part in range(2):
                        mm = pe.matmul(dst[:, off * D:(off + 1) * D],
                                       onehot[:, off, bass.ds(tile * P, P)], kvtab[:, b, part, col:col + D],
                                       start=(part == 0), stop=(part == 1))
                mm.then_inc(done, 1)

            def gather_k(u, t):
                n = 2 * u + t
                if first(n, 1):
                    pe.wait_ge(s_prod, n)
                gather(ps_k, 0, u, t, s_kp)

            def gather_v(u, t):
                n = 2 * u + t
                if first(n, 1):
                    pe.wait_ge(s_vc2, n)
                gather(ps_v, D, u, t, s_vp)

            def project(dst, src, w, done):
                for t in range(2):
                    for c in range(C):
                        mm = pe.matmul(dst[:, t * D:(t + 1) * D], src[:, c, t * P:(t + 1) * P], w[:, c, :],
                                       start=(c == 0), stop=(c == C - 1))
                mm.then_inc(done, 1)

            def attn_out(u, k):
                pe.wait_ge(s_oT, u + 1)
                if first(u, 1):
                    pe.wait_ge(s_x1, u)
                project(ps_y, oT[k], woT, s_yp)

            def transpose_xn2(u, k):
                pe.wait_ge(s_xn2, u + 1)
                if isinstance(u, int) and u + 5 > NP:
                    pe.wait_ge(s_xn2T, u)
                else:
                    pe.wait_ge(s_xT, u + 5)
                for t in range(2):
                    for c in range(C):
                        mm = pe.transpose(ps_t[:, c * 2 * P + t * P:c * 2 * P + (t + 1) * P], xn2[k][:, t, c * P:(c + 1) * P], ident[:])
                mm.then_inc(s_xn2Tp, 1)

            def transpose_x(u, k):
                pe.wait_ge(s_xn, u + 1)
                if first(u, 5):
                    pe.wait_ge(s_xn2T, u - 4)
                elif u:
                    pe.wait_ge(s_xT, u)
                for t in range(2):
                    for c in range(C):
                        mm = pe.transpose(ps_t[:, c * 2 * P + t * P:c * 2 * P + (t + 1) * P], xn[k][:, t, c * P:(c + 1) * P], ident[:])
                mm.then_inc(s_xTp, 1)

            def queries(u, k):
                pe.wait_ge(s_xT, u + 1)
                if first(u, 1):
                    pe.wait_ge(s_q, u)
                project(ps_q, xT[k], wqT, s_qp)

            def step(i, k, before_x=None):
                on = lambda lag: not isinstance(i, int) or lag <= i < NP + lag
                if on(2):
                    gather_v(i - 2, 0)
                if on(5):
                    transpose_xn2(i - 5, 1 - k)
                if on(3):
                    transpose_o(i - 3, 1 - k)
                if on(2):
                    gather_v(i - 2, 1)
                if on(1):
                    gather_k(i - 1, 1)
                if on(3):
                    attn_out(i - 3, 1 - k)
                if before_x:
                    before_x()
                if on(0):
                    transpose_x(i, k)
                    gather_k(i, 0)
                    queries(i, k)

            def win_T(hf):
                for f in range(FC // 2):
                    for c in range(C):
                        fc = hf * (FC // 2) + f
                        mm = pe.transpose(bank67[:, f * D + c * P:f * D + (c + 1) * P], win_ld[:, c, fc * P:(fc + 1) * P], ident[:])
                mm.then_inc(s_winTp, 1)

            transpose_x(0, 0)
            weight_T(ps_y, wo_ld, s_wo, s_woTp)
            pe.wait_ge(s_wqT, 1)
            queries(0, 0)
            pe.wait_ge(s_win, 16)
            pe.wait_ge(s_woT, 1)
            win_T(0)
            pe.wait_ge(s_oh, 1)
            pe.wait_ge(s_kvlo, 2)
            gather_k(0, 0)
            project_kv(2)
            project_kv(3)
            step(1, 1)
            pe.wait_ge(s_winq, 2)
            win_T(1)
            pe.wait_ge(s_kvlo, NB)

            def win_back():
                pe.wait_ge(s_winq, 4)
                w8p = bank67[:].bitcast(F16).rearrange("p (c f) -> p c f", c=C)
                for f in range(FC):
                    for c in range(C):
                        mm = pe.transpose(w8p[:, c, f * P:(f + 1) * P], win_f16[:, f, c * P:(c + 1) * P], ident16[:])
                mm.then_inc(s_w8p, 1)

            step(2, 0, before_x=win_back)
            pe.wait_ge(s_w8, 1)
            step(3, 1)
            for i in range(4, 6):
                pe.wait_ge(s_oh, i - 2)
                step(i, i % 2)
            pe.wait_ge(s_oh, NB)
            with pe.Fori(3, NP // 2) as j:
                for k in range(2):
                    step(2 * j + k, k)
            for i in range(NP, NP + 5):
                step(i, i % 2)

            pe.wait_ge(s_xn2T, NP)

            def expand(g, k):
                pe.wait_ge(s_xq, g + 1)
                for f in range(FC):
                    n = g * FC + f
                    if first(n, FC):
                        pe.wait_ge(s_h, g * FC + f - FC + 1)
                    bank = wide[f // 2 % 4][:, (f % 2) * 512:(f % 2) * 512 + GT]
                    at = 0
                    for c in range(C):
                        for part in (xhi, xlo):
                            mm = pe.matmul(bank, win8[:, c, f * P:(f + 1) * P], part[k][:, c, :],
                                           start=(at == 0), stop=(at == 2 * C - 1))
                            at += 1
                    mm.then_inc(s_z, 1)

            expand(0, 0)
            expand(1, 1)
            with pe.Fori(1, NG // 2) as j:
                for k in range(2):
                    expand(2 * j + k, k)

            pe.wait_ge(s_h, NG * FC)
            pe.wait_ge(s_wout8, 1)

            def contract(g, k):
                if first(g, 2):
                    pe.wait_ge(s_ys, 4 * g - 4)
                for f in range(FC):
                    for r, part in enumerate((hhi, hlo)):
                        if r == 1:
                            pe.wait_ge(s_hlo, g * FC + f + 1)
                        elif f in ON_ACT:
                            pe.wait_ge(s_hhia, g * len(ON_ACT) + ON_ACT.index(f) + 1)
                        else:
                            pe.wait_ge(s_hhi, g * (FC - len(ON_ACT)) + by_dve(f) + 1)
                        for t in range(4):
                            bank = wide[2 * k + t // 2][:, (t % 2) * 512:(t % 2) * 512 + D]
                            mm = pe.matmul(bank, part[f][:, t * P:(t + 1) * P], wout8[:, f, :],
                                           start=(f == 0 and r == 0), stop=(f == FC - 1 and r == 1))
                            if f == FC - 1 and r == 1:
                                mm.then_inc(s_acc, 1)
                            elif r == 1 and t == 3:
                                mm.then_inc(s_hused, 1)

            contract(0, 0)
            contract(1, 1)
            with pe.Fori(1, NG // 2) as j:
                for k in range(2):
                    contract(2 * j + k, k)

        @block.vector
        def _(dve):
            chain = [0]

            def link(ins):
                chain[0] += 1
                ins.then_inc(s_vc, 1)
                dve.wait_ge(s_vc, chain[0])

            def hold(u):
                if not isinstance(u, int):
                    dve.sem_inc(s_pace[0], 1)

            def stats(n, u, k):
                for t in range(2):
                    ins = dve.bn_stats(bn[n][k][:, t, :], xres[:, 2 * u + t, :])
                ins.then_inc(s_bn[n], 1)

            def aggregate(n, i, u, k):
                dve.wait_ge(s_bn[n], u + 1)
                hold(u)
                for t in range(2):
                    ins = dve.bn_aggr(mv[k][:, 2 * n + t, :], bn[n][k][:, t, :])
                if n == 1 or isinstance(i, int) and i < 4:
                    ins.then_inc(s_mv, 1)

            def norm_bias(i, k):
                at = slice(0 if not isinstance(i, int) or i < NP else 2, 4 if not isinstance(i, int) or i >= 4 else 2)
                dve.wait_ge(s_rstd, i + 1)
                dve.scalar_tensor_tensor(out=nbias[k][:, at], in0=mv[k][:, at, 0], scalar=-1.0, in1=rstd[k][:, at],
                                         op0=ALU.mult, op1=ALU.mult).then_inc(s_nb, 1)

            def qk(u, k, t):
                n = 2 * u + t
                dve.wait_ge(s_q, u + 1)
                dve.wait_ge(s_kp, n + 1)
                dve.tensor_tensor(prod[t][:], ps_k[:].rearrange("p (o d) -> p o d", o=KW),
                                  q[k][:, t, :].unsqueeze(1).broadcast_to([P, KW, D]), ALU.mult).then_inc(s_prod, 1)

            def qk_sum(u, k, t):
                n = 2 * u + t
                dve.wait_ge(s_prod, n + 1)
                dve.tensor_reduce(s[k][:, t].rearrange("p o h -> p (o h)"),
                                  prod[t][:].rearrange("p o (h d) -> p (o h) d", h=H), AX.X, ALU.add).then_inc(s_red, 1)

            def mask(u, k):
                s3 = s[k][:].rearrange("p t o h -> p (t o) h")
                dve.wait_ge(s_red, 2 * u + 2)
                dve.tensor_tensor(s3, s3, neg[:, bass.ds(2 * u, 2), :].rearrange("p t o -> p (t o)").unsqueeze(2)
                                  .broadcast_to([P, 2 * KW, H]), ALU.add).then_inc(s_masked, 1)

            def score_max(u, k):
                dve.wait_ge(s_masked, u + 1)
                dve.tensor_reduce(smax[k][:], s[k][:].rearrange("p t o h -> p t h o"), AX.X, ALU.max).then_inc(s_smax, 1)

            def shift(u, k):
                dve.wait_ge(s_smax, u + 1)
                dve.tensor_tensor(s[k][:], s[k][:], smax[k][:].unsqueeze(2).broadcast_to([P, 2, KW, H]),
                                  ALU.subtract).then_inc(s_shift, 1)

            def exp_sum(u, k):
                dve.wait_ge(s_exp, u + 1)
                dve.tensor_reduce(ssum[k][:], e[k][:].rearrange("p t o h -> p t h o"), AX.X, ALU.add).then_inc(s_ssum, 1)

            def inv_sum(u, k):
                dve.wait_ge(s_ssum, u + 1)
                dve.reciprocal(srec[k][:], ssum[k][:]).then_inc(s_srec, 1)

            def probs(u, k):
                dve.wait_ge(s_srec, u + 1)
                if first(u, 2):
                    dve.wait_ge(s_pv, 2 * u - 2)
                dve.tensor_tensor(pr[k][:], e[k][:], srec[k][:].unsqueeze(2).broadcast_to([P, 2, KW, H]),
                                  ALU.mult).then_inc(s_p, 1)

            def residual(u, k):
                xv = xres[:, bass.ds(2 * u, 2), :].rearrange("p t d -> p (t d)")
                dve.wait_ge(s_yp, u + 1)
                hold(u)
                dve.scalar_tensor_tensor(out=xv, in0=ps_y, scalar=tanhs[:, 0:1], in1=xv, op0=ALU.mult,
                                         op1=ALU.add).then_inc(s_x1, 1)

            def largest(u, k):
                dve.wait_ge(s_xn2, u + 1)
                hold(u)
                dve.tensor_reduce(xmax[:, bass.ds(u, 1)], xn2[k][:].rearrange("p t d -> p (t d)"), AX.X, ALU.max,
                                  apply_absolute_value=True).then_inc(s_xmax, 1)

            def step(i, k):
                on = lambda lag: not isinstance(i, int) or lag <= i < NP + lag
                if on(0):
                    stats(0, i, k)
                if on(4):
                    dve.wait_ge(s_x1, i - 3)
                    hold(i)
                    stats(1, i - 4, k)
                if on(2):
                    exp_sum(i - 2, k)
                if on(0):
                    aggregate(0, i, i, k)
                if on(4):
                    aggregate(1, i, i - 4, k)
                if on(2):
                    inv_sum(i - 2, k)
                    probs(i - 2, k)
                if on(1):
                    qk(i - 1, 1 - k, 0)
                if not isinstance(i, int) or i < NP + 4:
                    norm_bias(i, k)
                if on(1):
                    qk_sum(i - 1, 1 - k, 0)
                    qk(i - 1, 1 - k, 1)
                    qk_sum(i - 1, 1 - k, 1)
                if on(5):
                    largest(i - 5, 1 - k)
                if on(1):
                    mask(i - 1, 1 - k)
                if on(3):
                    residual(i - 3, 1 - k)
                if on(1):
                    score_max(i - 1, 1 - k)
                    shift(i - 1, 1 - k)

            def clamp_seg(b):
                dve.wait_ge(s_segb[b], 16)
                link(dve.tensor_scalar(seg_b[:, b * LQ:(b + 1) * LQ].rearrange("u (t p) -> u t p", t=TB),
                                       seg_i[:, b * LQ:(b + 1) * LQ].rearrange("u (p t) -> u t p", t=TB),
                                       float(U - 1), 0.0, ALU.min, ALU.max))

            def make_onehot(b):
                for off in range(KW):
                    ins = dve.tensor_scalar(onehot[:, off, b * LQ:(b + 1) * LQ], seg_b[:, b * LQ:(b + 1) * LQ],
                                            jo[:, off:off + 1], kvp[:, 3, b:b + 1], ALU.is_equal, ALU.mult)
                ins.then_inc(s_oh, 1)

            def kv_scales(b):
                v = slice(b, b + 2)
                dve.wait_ge(s_kv, b + 2)
                link(dve.tensor_reduce(kvp[:, 0, v], bank23[0:U, :].rearrange("u (b n) -> u b n", b=2), AX.X, ALU.max,
                                       apply_absolute_value=True))
                link(dve.tensor_scalar(kvp[:, 0, v], kvp[:, 0, v], 2.0 ** -96, None, ALU.max))
                link(dve.tensor_scalar(kvp[:, 1, v].bitcast(I32), kvp[:, 0, v].bitcast(I32), POW2_BITS, None, ALU.bitwise_and))
                link(dve.tensor_scalar(kvp[:, 3, v], kvp[:, 1, v], 1.0 / HALF_TOP, None, ALU.mult))
                dve.reciprocal(kvp[:, 2, v], kvp[:, 3, v]).then_inc(s_kvscale, 1)
                dve.wait_ge(s_kvscale, b // 2 + 1)

            def kv_low(b):
                dve.wait_ge(s_kvhi, b + 1)
                t, c0 = kv_ap[b]
                dve.scalar_tensor_tensor(out=kvtab[:, b, 1, :], in0=t[0:U, c0:c0 + 2 * D], scalar=kvp[:, 2, b:b + 1],
                                         in1=kvtab[:, b, 0, :], op0=ALU.mult, op1=ALU.subtract).then_inc(s_kvlo, 1)

            def win_scales(hf):
                v = slice(hf * FC // 2, (hf + 1) * FC // 2)
                dve.wait_ge(s_winTp, hf + 1)
                link(dve.tensor_reduce(amax_win[:, v], bank67[:].rearrange("p (f d) -> p f d", f=FC // 2), AX.X, ALU.max,
                                       apply_absolute_value=True))
                link(dve.tensor_scalar(amax_win[:, v], amax_win[:, v], AMAX_FLOOR, None, ALU.max))
                link(dve.reciprocal(sc_win[:, v], amax_win[:, v]))
                dve.tensor_scalar(sc_win[:, v], sc_win[:, v], W_LEVELS, None, ALU.mult).then_inc(s_winsc, 1)

            dve.wait_ge(s_wkvTp, 1)
            dve.tensor_copy(wkvT[:].rearrange("p c e -> p (c e)"), bank45[:]).then_inc(s_wkvT, 1)
            dve.wait_ge(s_x[0], 16)
            stats(0, 0, 0)
            aggregate(0, 0, 0, 0)
            dve.wait_ge(s_jo, 1)
            clamp_seg(0)
            norm_bias(0, 0)
            dve.wait_ge(s_segt, 16)
            link(dve.tensor_scalar(seg_f[:], seg_t[:], 0.0, None, ALU.max))
            for off in range(KW):
                ins = dve.tensor_scalar(neg[:, :, off], seg_f[:], float(off), NEG, ALU.is_lt, ALU.mult)
            ins.then_inc(s_neg, 1)
            kv_scales(0)
            make_onehot(0)
            kv_low(0)
            kv_low(1)
            clamp_seg(1)
            make_onehot(1)
            win_scales(0)
            dve.wait_ge(s_neg, 1)
            kv_scales(2)
            step(1, 1)
            kv_low(2)
            kv_low(3)
            win_scales(1)
            step(2, 0)
            clamp_seg(2)
            make_onehot(2)
            dve.wait_ge(s_tanh, 1)
            step(3, 1)
            for b in range(3, NB):
                clamp_seg(b)
                make_onehot(b)
            for b in range(1, NB):
                dve.wait_ge(s_x[b], 16)
            for i in range(4, 6):
                step(i, i % 2)
            with dve.Fori(3, NP // 2) as j:
                for k in range(2):
                    step(2 * j + k, k)
            for i in range(NP, NP + 5):
                step(i, i % 2)

            dve.wait_ge(s_xmax, NP)
            dve.tensor_reduce(qx[:, 0:1], xmax[:], AX.X, ALU.max).then_inc(s_xall, 1)
            dve.tensor_scalar(bout[:], bout[:], tanhs[:, 1:2], None, ALU.mult).then_inc(s_bias, 1)
            dve.wait_ge(s_qxr, 1)
            link(dve.tensor_scalar(qx[:, 2:3], qx[:, 1:2], AMAX_FLOOR, 1.0 / A_LEVELS, ALU.max, ALU.mult))
            link(dve.reciprocal(qx[:, 3:4], qx[:, 2:3]))

            def quantise_x(g, k):
                n = 2 if isinstance(g, int) and g < 2 else 0
                if not n:
                    dve.wait_ge(s_z, (g - 1) * FC)
                    hold(g)
                dve.tensor_scalar(xr[k][:], xn2T[:, g, :, :], qx[:, 3:4], None, ALU.mult).then_inc(s_xr, 1)
                dve.wait_ge(s_xr, g + 1)
                dve.tensor_copy(xhi[k][:], xr[k][:]).then_inc(s_xhi, 1)
                dve.wait_ge(s_xhi, g + 1)
                dve.tensor_tensor(xlo[k][:], xr[k][:], xhi[k][:], ALU.subtract).then_inc(s_xq, 1)

            def hidden_max(g, m):
                dve.wait_ge(s_h, g * FC + 2 * m + 2)
                hold(g)
                dve.tensor_reduce(hmax[:, bass.ds(g * (FC // 2) + m, 1)], hidden[:, g, 2 * m:2 * m + 2, :], AX.XY, ALU.max,
                                  apply_absolute_value=True).then_inc(s_hm, 1)

            def stage_b(g, k, last=False):
                hidden_max(g, 0)
                hidden_max(g, 1)
                if not last:
                    quantise_x(g + 1, 1 - k)
                hidden_max(g, 2)
                hidden_max(g, 3)

            quantise_x(0, 0)
            link(dve.tensor_scalar(qx[:, 4:5], qx[:, 2:3], 1.0 / W_LEVELS, None, ALU.mult))
            dve.tensor_scalar(zscale[:], amax_win[:], qx[:, 4:5], None, ALU.mult).then_inc(s_qxs, 1)
            dve.wait_ge(s_wout, 16)
            link(dve.tensor_reduce(amax_wout[:], wout_ld[:], AX.X, ALU.max, apply_absolute_value=True))
            link(dve.tensor_scalar(amax_wout[:], amax_wout[:], AMAX_FLOOR, None, ALU.max))
            dve.tensor_reduce(top_wout[:, 0:1], amax_wout[:], AX.X, ALU.max).then_inc(s_wrow, 1)
            link(dve.reciprocal(sc_wout[:], amax_wout[:]))
            link(dve.tensor_scalar(sc_wout[:], sc_wout[:], W_LEVELS, None, ALU.mult))
            for f in range(FC):
                ins = dve.tensor_scalar(w_i16[:, f, :], wout_ld[:, f, :], sc_wout[:, f:f + 1], None, ALU.mult)
            link(ins)
            dve.tensor_copy(wout8[:], w_i16[:]).then_inc(s_wout8, 1)
            stage_b(0, 0)
            dve.wait_ge(s_wall, 1)
            link(dve.reciprocal(top_wout[:, 2:3], top_wout[:, 1:2]))
            dve.tensor_scalar(rel_wout[:], amax_wout[:], top_wout[:, 2:3], None, ALU.mult).then_inc(s_rel, 1)
            link(dve.tensor_scalar(qh[:, 4:5], top_wout[:, 1:2], tanhs[:, 1:2], 1.0 / W_LEVELS, ALU.mult, ALU.mult))
            stage_b(1, 1)
            with dve.Fori(1, NG // 2 - 1) as j:
                for k in range(2):
                    stage_b(2 * j + k, k)
            stage_b(NG - 2, 0)
            stage_b(NG - 1, 1, last=True)

            dve.wait_ge(s_hm, NG * FC // 2)
            dve.tensor_reduce(qh[:, 0:1], hmax[:], AX.X, ALU.max).then_inc(s_hall, 1)
            dve.wait_ge(s_qhr, 1)
            link(dve.tensor_scalar(qh[:, 2:3], qh[:, 1:2], AMAX_FLOOR, 1.0 / A_LEVELS, ALU.max, ALU.mult))
            dve.reciprocal(qh[:, 3:4], qh[:, 2:3]).then_inc(s_qhs, 1)
            dve.tensor_scalar(qh[:, 5:6], qh[:, 2:3], qh[:, 4:5], None, ALU.mult).then_inc(s_qhs, 1)
            dve.wait_ge(s_rel, 1)

            def high(g, f):
                if f % 2 == 0:
                    dve.wait_ge(s_hq, g * (FC // 2) + f // 2 + 1)
                if f in ON_ACT:
                    return
                if first(g, 1):
                    dve.wait_ge(s_hused, (g - 1) * (FC - 1) + f + 1)
                dve.tensor_scalar(hhi[f][:], hq[f // 2][:, f % 2, :], rel_wout[:, f:f + 1], None,
                                  ALU.mult).then_inc(s_hhi, 1)

            def low(g, f):
                if f in ON_ACT:
                    dve.wait_ge(s_hhia, g * len(ON_ACT) + ON_ACT.index(f) + 1)
                else:
                    dve.wait_ge(s_hhi, g * (FC - len(ON_ACT)) + by_dve(f) + 1)
                dve.scalar_tensor_tensor(out=hlo[f][:], in0=hq[f // 2][:, f % 2, :], scalar=rel_wout[:, f:f + 1],
                                         in1=hhi[f][:], op0=ALU.mult, op1=ALU.subtract).then_inc(s_hlo, 1)

            def split_h(g):
                high(g, 0)
                for f in range(1, FC):
                    high(g, f)
                    low(g, f - 1)
                low(g, FC - 1)

            split_h(0)
            with dve.Fori(1, NG) as g:
                split_h(g)


_INS = ["x", "ctx_1024", "itok_BxS_0_511", "g_xattn", "g_ffn", "L0_xattn_Wq", "L0_xattn_Wkv", "L0_xattn_Wo",
        "L0_ffn_W_in", "L0_ffn_b_in", "L0_ffn_W_out", "L0_ffn_b_out"]


def kernel(**inputs):
    import numpy as _np
    import concourse.bacc as _bacc
    from concourse import mybir as _mybir
    from concourse.bass_utils import run_bass_kernel_spmd as _run

    nc = _bacc.Bacc("TRN2", target_bir_lowering=False, num_devices=1)
    arrays, args = {}, []
    for name in _INS:
        a = _np.ascontiguousarray(inputs[name])
        arrays[f"in_{name}_dram"] = a
        args.append(nc.dram_tensor(f"in_{name}_dram", a.shape, _mybir.dt.from_np(a.dtype), kind="ExternalInput").ap())
    out = nc.dram_tensor("out_dram", arrays["in_x_dram"].shape, _mybir.dt.float32, kind="ExternalOutput").ap()
    flamingo_kernel(nc, *args, out)
    r = _run(nc, [arrays], core_ids=[0])
    return r.results[0]["out_dram"]
```
